# Optimizing a Trainium2 kernel written in Bass

```python
import numpy as np
import jax
import jax.numpy as jnp

def _softmax(x, axis=-1):
    return jax.nn.softmax(x, axis=axis)

def _gelu(x):
    return jax.nn.gelu(x, approximate=True)

def _silu(x):
    return jax.nn.silu(x)

def _sigmoid(x):
    return jax.nn.sigmoid(x)

def _layernorm(x, axis=-1, eps=1e-05):
    m = jnp.mean(x, axis=axis, keepdims=True)
    v = jnp.var(x, axis=axis, keepdims=True)
    return (x - m) / jnp.sqrt(v + eps)

def _scatter_add(tgt, idx, src, axis=0):
    return tgt.at[idx].add(src)

def _segment_sum(src, seg, n):
    return jax.ops.segment_sum(src, seg, n)
kernel_name = 'mk_adaln_ffn_d1_seqx_r8_ed85ca'

def setup_inputs(seed: int=0):
    np.random.seed(seed)
    _w = jnp.asarray

    def _rec_inputs():
        import jax
        import jax.numpy as jnp
        _rk = jax.random.key(seed)
        x = -1.394e-06 + 0.9999 * jax.random.normal(jax.random.fold_in(_rk, 1), (32, 32, 256), jnp.float32)
        _lenS = 32 - jax.random.randint(jax.random.fold_in(_rk, 7), (32,), 0, max(1, 32 // 4) + 1, jnp.int32)
        _lenS2 = 32 - jax.random.randint(jax.random.fold_in(_rk, 8), (32,), 0, max(1, 32 // 4) + 1, jnp.int32)
        cond_2048 = -0.00499425 + 1.0058 * jax.random.normal(jax.random.fold_in(_rk, 11), (32, 256), jnp.float32)
        return (x, cond_2048)
    x, cond_2048 = _rec_inputs()

    def _L0_cond_setup():
        import jax, jax.numpy as jnp
        import numpy as np
        B, T, D = (16, 128, 256)
        key = jax.random.key(seed)
        k0, k1, k2, k3 = jax.random.split(key, 4)
        scale = 1.0 / np.sqrt(D)
        return {'initial_state': jax.random.normal(k0, (B, D), jnp.float32), 'inputs': jax.random.normal(k1, (B, T, D), jnp.float32), 'W_ih': jax.random.normal(k2, (D, 3 * D), jnp.float32) * scale, 'W_hh': jax.random.normal(k3, (D, 3 * D), jnp.float32) * scale, 'b_ih': jnp.zeros((3 * D,), jnp.float32), 'b_hh': jnp.zeros((3 * D,), jnp.float32)}
    _L0_cond_all = _L0_cond_setup()
    _L0_cond_in = {k: v for k, v in _L0_cond_all.items() if k in ('W_ih', 'W_hh', 'b_ih', 'b_hh')}
    del _L0_cond_all

    def _L0_ffn_setup():
        import jax, jax.numpy as jnp
        import numpy as np
        H = 256
        I = 128
        K = 8
        E = 128
        TOPK = 4
        EPS = 1e-08
        key = jax.random.key(seed)
        ks = jax.random.split(key, 10)
        s = 0.02
        return {'x': jax.random.normal(ks[0], (4, 256, H), jnp.float32), 'w_router': jax.random.normal(ks[1], (H, E), jnp.float32) * s, 'w_gate': jax.random.normal(ks[2], (H, K * I), jnp.float32) * s, 'w_up': jax.random.normal(ks[3], (H, K * I), jnp.float32) * s, 'w_down': jax.random.normal(ks[4], (I, H), jnp.float32) * s, 'amplitudes': jax.random.normal(ks[5], (E, K, 2), jnp.float32) * 0.1, 'expert_scale': jnp.ones((E,), jnp.float32), 'shared_w_gate': jax.random.normal(ks[6], (H, 2 * I), jnp.float32) * s, 'shared_w_up': jax.random.normal(ks[7], (H, 2 * I), jnp.float32) * s, 'shared_w_down': jax.random.normal(ks[8], (2 * I, H), jnp.float32) * s}
    _L0_ffn_all = _L0_ffn_setup()
    _L0_ffn_in = {k: v for k, v in _L0_ffn_all.items() if k in ('w_router', 'w_gate', 'w_up', 'w_down', 'amplitudes', 'expert_scale', 'shared_w_gate', 'shared_w_up', 'shared_w_down')}
    del _L0_ffn_all
    return {'x': x, 'cond_2048': cond_2048, 'L0_cond_W_ih': _L0_cond_in['W_ih'], 'L0_cond_W_hh': _L0_cond_in['W_hh'], 'L0_cond_b_ih': _L0_cond_in['b_ih'], 'L0_cond_b_hh': _L0_cond_in['b_hh'], 'L0_ffn_w_router': _L0_ffn_in['w_router'], 'L0_ffn_w_gate': _L0_ffn_in['w_gate'], 'L0_ffn_w_up': _L0_ffn_in['w_up'], 'L0_ffn_w_down': _L0_ffn_in['w_down'], 'L0_ffn_amplitudes': _L0_ffn_in['amplitudes'], 'L0_ffn_expert_scale': _L0_ffn_in['expert_scale'], 'L0_ffn_shared_w_gate': _L0_ffn_in['shared_w_gate'], 'L0_ffn_shared_w_up': _L0_ffn_in['shared_w_up'], 'L0_ffn_shared_w_down': _L0_ffn_in['shared_w_down']}

def reference(x, cond_2048, L0_cond_W_ih, L0_cond_W_hh, L0_cond_b_ih, L0_cond_b_hh, L0_ffn_w_router, L0_ffn_w_gate, L0_ffn_w_up, L0_ffn_w_down, L0_ffn_amplitudes, L0_ffn_expert_scale, L0_ffn_shared_w_gate, L0_ffn_shared_w_up, L0_ffn_shared_w_down):
    import jax
    import jax.numpy as jnp

    def _L0_cond_ref(initial_state, inputs, W_ih, W_hh, b_ih, b_hh):
        import jax, jax.numpy as jnp
        import numpy as np
        B, T, D = (16, 128, 256)
        "ScanOverTime(GRU cell): sequential per-timestep module call with\n            dict-state passing; merge_dict_trees stacks the per-step\n            'state_predicted' tensors along axis=1 -> [B, T, D]."

        def cell(h, x):
            gi = x @ W_ih + b_ih
            gh = h @ W_hh + b_hh
            i_r, i_z, i_n = jnp.split(gi, 3, axis=-1)
            h_r, h_z, h_n = jnp.split(gh, 3, axis=-1)
            r = jax.nn.sigmoid(i_r + h_r)
            z = jax.nn.sigmoid(i_z + h_z)
            n = jnp.tanh(i_n + r * h_n)
            h_new = (1.0 - z) * n + z * h
            return (h_new, h_new)
        xs = jnp.swapaxes(inputs, 0, 1)
        _, hs = jax.lax.scan(cell, initial_state, xs)
        return jnp.swapaxes(hs, 0, 1)

    def _L0_ffn_ref(x, w_router, w_gate, w_up, w_down, amplitudes, expert_scale, shared_w_gate, shared_w_up, shared_w_down):
        import jax, jax.numpy as jnp
        import numpy as np
        H = 256
        I = 128
        K = 8
        E = 128
        TOPK = 4
        EPS = 1e-08
        B, S, _ = x.shape
        T = B * S
        xt = x.reshape(T, H)
        probs = jax.nn.softmax(xt @ w_router, axis=-1)
        topk_p, topk_idx = jax.lax.top_k(probs, TOPK)
        topk_w = topk_p / (jnp.sum(topk_p, axis=-1, keepdims=True) + EPS)
        gate = (xt @ w_gate).reshape(T, K, I)
        up = (xt @ w_up).reshape(T, K, I)
        basis = jax.nn.silu(gate) * up
        p = amplitudes[..., 0] ** 2 + amplitudes[..., 1] ** 2
        mix = p / (jnp.sum(p, axis=-1, keepdims=True) + EPS)
        mix_sel = mix[topk_idx]
        mixed = jnp.einsum('tek,tki->tei', mix_sel, basis)
        down = jnp.einsum('tei,ih->teh', mixed, w_down)
        coeff = topk_w * expert_scale[topk_idx]
        out = jnp.einsum('teh,te->th', down, coeff)
        shared = jax.nn.silu(xt @ shared_w_gate) * (xt @ shared_w_up) @ shared_w_down
        out = out + shared
        return out.reshape(B, S, H)
    x = x + _L0_ffn_ref(_L0_cond_ref(cond_2048, x, L0_cond_W_ih, L0_cond_W_hh, L0_cond_b_ih, L0_cond_b_hh), L0_ffn_w_router, L0_ffn_w_gate, L0_ffn_w_up, L0_ffn_w_down, L0_ffn_amplitudes, L0_ffn_expert_scale, L0_ffn_shared_w_gate, L0_ffn_shared_w_up, L0_ffn_shared_w_down)
    return x

_drawn_inputs = setup_inputs


def setup_inputs(seed=0):
    import zlib

    import numpy as np

    out = dict(_drawn_inputs(seed))
    spreads = {'L0_cond_b_ih': (0.0, 0.8), 'L0_cond_b_hh': (0.0, 0.8), 'L0_ffn_expert_scale': (1.0, 0.6)}
    factors = {'cond_2048': 8.0,
     'L0_cond_W_ih': 8.0,
     'L0_cond_W_hh': 8.0,
     'L0_ffn_w_router': 8.0,
     'L0_ffn_w_gate': 8.0,
     'L0_ffn_w_up': 8.0,
     'L0_ffn_w_down': 8.0,
     'L0_ffn_amplitudes': 8.0,
     'L0_ffn_shared_w_gate': 8.0,
     'L0_ffn_shared_w_up': 8.0,
     'L0_ffn_shared_w_down': 8.0}
    for name, (base, spread) in spreads.items():
        noise = np.random.default_rng([zlib.crc32(name.encode()), seed]).standard_normal(out[name].shape)
        drawn = base * np.exp(spread * noise) if base else spread * noise
        out[name] = jnp.asarray(drawn.astype(out[name].dtype))
    for name, factor in factors.items():
        out[name] = (out[name] * factor).astype(out[name].dtype)
    return out
```

```python
from contextlib import ExitStack

import concourse.bass as bass
from concourse import mybir

F32 = mybir.dt.float32
F32R = mybir.dt.float32r
BF16 = mybir.dt.bfloat16
ALU = mybir.AluOpType
ACT = mybir.ActivationFunctionType

B, T, D = 32, 32, 256
P = 128
Q = 32
NJ = P // Q
FJ = D // NJ
KB = D // P
TC = P // B
NC = T // TC
E, K, I = 128, 8, 128
TOPK, EPS = 4, 1e-8
UW = 256
NU = K * I // UW + 1
ROUTER = 2 * UW * NU
WCOLS = ROUTER + E
NB = 3
LOWEST, HIGHEST = -3.0e38, 3.0e38
HN, R, Z, IN = 0, FJ, 2 * FJ, 3 * FJ


def build(nc, x, cond, w_ih, w_hh, b_ih, b_hh, w_router, w_gate, w_up, w_down, amplitudes, expert_scale,
          sw_gate, sw_up, sw_down, out):
    with ExitStack() as ctx:
        def sb(name, shape, dt=F32):
            return ctx.enter_context(nc.sbuf_tensor(name, shape, dt))

        def bank(name):
            return ctx.enter_context(nc.psum_tensor(name, [P, 512], F32))

        def sem(name):
            return ctx.enter_context(nc.semaphore(name))

        whh = sb("whh", [P, KB, 3 * D])
        wih = sb("wih", [P, KB, 3 * D])
        wraw = sb("wraw", [P, KB, WCOLS])
        whi = sb("whi", [P, KB, WCOLS], F32R)
        wlo = sb("wlo", [P, KB, WCOLS], F32R)
        draw = sb("draw", [P, 3, D])
        dhi_w = sb("dhi_w", [P, 3, D], F32R)
        dlo_w = sb("dlo_w", [P, 3, D], F32R)
        bi4 = sb("bi4", [NJ, 3, FJ])
        bh4 = sb("bh4", [NJ, 3, FJ])
        bsum = sb("bsum", [NJ, 3, 4 * FJ])
        bpart = sb("bpart", [NJ, 3, 4 * FJ], BF16)
        bias3 = sb("bias3", [P, 4 * FJ], BF16)
        pick = sb("pick", [P, NJ, Q], BF16)
        ident = sb("ident", [P, P])
        amp = sb("amp", [P, K, 2])
        amp2 = sb("amp2", [P, K, 2])
        pk = sb("pk", [P, K])
        psum_k = sb("psum_k", [P, 1])
        prec = sb("prec", [P, 1])
        scale_e = sb("scale_e", [P, 1])
        mix = sb("mix", [P, K])
        xj = sb("xj", [P, T, FJ])
        xT = sb("xT", [P, T, FJ])
        xtok = sb("xtok", [P, NC, D])
        h0 = sb("h0", [P, FJ])
        hT0 = sb("hT0", [P, FJ])
        hT = sb("hT", [P, 2, KB, TC, B])
        hThi = sb("hThi", [P, 2, KB, TC, B], F32R)
        hTlo = sb("hTlo", [P, 2, KB, TC, B], F32R)
        hhalf = sb("hhalf", [P, FJ])
        trz = sb("trz", [P, 2 * FJ])
        m = sb("m", [P, FJ])
        pre = sb("pre", [P, FJ])
        sc_mul = sb("sc_mul", [P, FJ, 2])
        sc_add = sb("sc_add", [P, FJ, 2])
        sc_out = sb("sc_out", [P, FJ, 2])
        th = sb("th", [P, 2, UW])
        p1 = sb("p1", [P, 2, UW])
        q = sb("q", [P, 2, K * I])
        shared = sb("shared", [P, 2, 2 * I])
        lx = sb("lx", [P, E + TOPK])
        v8 = sb("v8", [P, 8])
        keys = sb("keys", [P, 8])
        negmax = sb("negmax", [P, 1])
        ex = sb("ex", [P, E])
        exsum = sb("exsum", [P, 1])
        marked = sb("marked", [P, E + TOPK])
        em = sb("em", [P, E])
        sum4 = sb("sum4", [P, 1])
        den = sb("den", [P, 1])
        rec = sb("rec", [P, 1])
        emT = sb("emT", [P, P])
        coef = sb("coef", [P, 2, K])
        qc = sb("qc", [P, K * I])
        half = sb("half", [P, 4 * I])
        quarter = sb("quarter", [P, 2 * I])
        mixed = sb("mixed", [P, I])
        dhi = sb("dhi", [P, 3, P], F32R)
        dlo = sb("dlo", [P, 3, P], F32R)
        ot = sb("ot", [P, 2, D])

        gates = [bank("gates0"), bank("gates1")]
        unit_bank = [bank(f"unit{n}") for n in range(NB)]
        route = bank("route")
        turned = bank("turned")
        down = bank("down")
        LOGITS, EMT, COEF = slice(0, E), slice(E, 2 * E), slice(2 * E, 2 * E + K)

        ld_rec = sem("ld_rec")
        ld_x0 = sem("ld_x0")
        ld_x1 = sem("ld_x1")
        ld_xtok = sem("ld_xtok")
        ld_mix = sem("ld_mix")
        ld_unit = [sem(f"ld_unit{u}") for u in range(NU)]
        ld_router = sem("ld_router")
        ld_down = sem("ld_down")
        const_ready = sem("const_ready")
        whh_scaled = sem("whh_scaled")
        bias_step = sem("bias_step")
        mix_step = sem("mix_step")
        x_turned = sem("x_turned")
        w_hi = sem("w_hi")
        w_lo = sem("w_lo")
        gates_ready = sem("gates_ready")
        rz_ready = sem("rz_ready")
        m_ready = sem("m_ready")
        pre_ready = sem("pre_ready")
        n_ready = sem("n_ready")
        blend_ready = sem("blend_ready")
        h_ready = sem("h_ready")
        hT_ready = sem("hT_ready")
        hhalf_ready = sem("hhalf_ready")
        hThi_ready = sem("hThi_ready")
        hTlo_ready = sem("hTlo_ready")
        logits_ready = sem("logits_ready")
        unit_ready = sem("unit_ready")
        th_ready = sem("th_ready")
        p1_ready = sem("p1_ready")
        q_ready = sem("q_ready")
        topk_step = sem("topk_step")
        ex_ready = sem("ex_ready")
        emT_turned = sem("emT_turned")
        emT_ready = sem("emT_ready")
        coef_psum = sem("coef_psum")
        coef_ready = sem("coef_ready")
        pool_mix = sem("pool_mix")
        turned_ready = sem("turned_ready")
        dhi_ready = sem("dhi_ready")
        dlo_ready = sem("dlo_ready")
        down_ready = sem("down_ready")
        out_ready = sem("out_ready")
        stored = [sem("stored0"), sem("stored1")]

        TOPK_STEPS = 8
        SPLITS = NU + 2
        block = ctx.enter_context(nc.Block())

        def rows(w, j):
            return w[FJ * j:FJ * (j + 1), :].rearrange("(s c) n -> c s n", s=KB)

        @block.sync
        def _(sp):
            for j in range(NJ):
                quad = slice(Q * j, Q * (j + 1))
                sp.dma_start(xj[quad, 0:TC, :], x[:, 0:TC, FJ * j:FJ * (j + 1)]).then_inc(ld_x0, 16)
                src = rows(w_ih, j)
                sp.dma_start(wih[quad, :, :], src).then_inc(ld_rec, 16)
            for j in range(NJ):
                quad = slice(Q * j, Q * (j + 1))
                src = rows(w_hh, j)
                sp.dma_start(whh[quad, :, 0:D], src[:, :, 2 * D:3 * D]).then_inc(ld_rec, 16)
                sp.dma_start(whh[quad, :, D:3 * D], src[:, :, 0:2 * D]).then_inc(ld_rec, 16)
            for j in range(NJ):
                quad = slice(Q * j, Q * (j + 1))
                sp.dma_start(xj[quad, TC:T, :], x[:, TC:T, FJ * j:FJ * (j + 1)]).then_inc(ld_x1, 16)
            for j in range(NJ):
                sp.dma_start(wraw[Q * j:Q * (j + 1), :, ROUTER:WCOLS], rows(w_router, j)).then_inc(ld_router, 16)
            for u in range(NU):
                g, up, at = (w_gate, w_up, UW * u) if u < NU - 1 else (sw_gate, sw_up, 0)
                for j in range(NJ):
                    quad = slice(Q * j, Q * (j + 1))
                    c0 = 2 * UW * u
                    sp.dma_start(wraw[quad, :, c0:c0 + UW], rows(g, j)[:, :, at:at + UW]).then_inc(ld_unit[u], 16)
                    sp.dma_start(wraw[quad, :, c0 + UW:c0 + 2 * UW], rows(up, j)[:, :, at:at + UW])\
                        .then_inc(ld_unit[u], 16)
            sp.dma_start(draw[:, 0, :], w_down).then_inc(ld_down, 16)
            sp.dma_start(draw[:, 1:3, :], sw_down.rearrange("(s p) n -> p s n", p=P)).then_inc(ld_down, 16)
            for t in range(TC):
                sp.dma_start(xtok[Q * t:Q * (t + 1), :, :],
                             x.rearrange("b (c t) d -> t b c d", t=TC)[t]).then_inc(ld_xtok, 16)
            for p in range(NC):
                sp.wait_ge(out_ready, p + 1)
                for t in range(TC):
                    sp.dma_start(out[:, TC * p + t, :], ot[Q * t:Q * (t + 1), p % 2, :])\
                        .then_inc(stored[p % 2], 16)
            for parity in range(2):
                sp.wait_ge(stored[parity], 16 * TC * (NC // 2))

        @block.gpsimd
        def _(pool):
            pool.memset(pick[:, :, :], 0.0).then_inc(const_ready, 1)
            pool.memset(bias3[:, :], 0.0).then_inc(const_ready, 1)
            pool.memset(ident[:, :], 0.0).then_inc(const_ready, 1)
            pool.memset(sc_mul[:, :, :], 0.0).then_inc(const_ready, 1)
            pool.memset(lx[:, E:E + TOPK], LOWEST).then_inc(const_ready, 1)
            pool.memset(keys[:, TOPK:8], LOWEST).then_inc(const_ready, 1)
            pool.wait_ge(const_ready, 3)
            for a in range(3):
                pool.affine_select(out=pick[:, :, :], in_=pick[:, :, :], compare_op=ALU.not_equal, fill=1.0,
                                   base=-Q * a, pattern=[[-1, NJ], [0, Q]], channel_multiplier=1)\
                    .then_inc(const_ready, 1)
                pool.wait_ge(const_ready, 7 + a)
            pool.affine_select(out=ident[:, :], in_=ident[:, :], compare_op=ALU.not_equal, fill=1.0,
                               base=0, pattern=[[-1, P]], channel_multiplier=1).then_inc(const_ready, 1)

            def halves(t):
                c, k = t // TC, t % TC
                pool.wait_ge(hT_ready, t + 2)
                if k == 0 and c >= 2:
                    pool.wait_ge(unit_ready, NU * (c - 1))
                pool.tensor_copy(hThi[:, c % 2, :, k, :], hT[:, c % 2, :, k, :]).then_inc(hThi_ready, 1)
                pool.wait_ge(hThi_ready, t + 1)
                pool.tensor_tensor(hTlo[:, c % 2, :, k, :], hT[:, c % 2, :, k, :],
                                   hThi[:, c % 2, :, k, :].bitcast(F32), ALU.subtract).then_inc(hTlo_ready, 1)

            def mix_basis(p):
                pool.wait_ge(coef_ready, p + 1)
                pool.wait_ge(q_ready, NU * p + NU - 1)
                pool.tensor_tensor(qc[:, :].rearrange("p (k i) -> p k i", k=K),
                                   q[:, p % 2, :].rearrange("p (k i) -> p k i", k=K),
                                   coef[:, p % 2, :].rearrange("p (k o) -> p k o", o=1).to_broadcast([P, K, I]),
                                   ALU.mult).then_inc(pool_mix, 1)
                pool.wait_ge(pool_mix, 4 * p + 1)
                pool.tensor_tensor(half[:, :], qc[:, 0:4 * I], qc[:, 4 * I:8 * I], ALU.add).then_inc(pool_mix, 1)
                pool.wait_ge(pool_mix, 4 * p + 2)
                pool.tensor_tensor(quarter[:, :], half[:, 0:2 * I], half[:, 2 * I:4 * I], ALU.add)\
                    .then_inc(pool_mix, 1)
                pool.wait_ge(pool_mix, 4 * p + 3)
                if p >= 1:
                    pool.wait_ge(turned_ready, p)
                pool.tensor_tensor(mixed[:, :], quarter[:, 0:I], quarter[:, I:2 * I], ALU.add)\
                    .then_inc(pool_mix, 1)

            for t in range(T):
                halves(t)
                if t % TC == 0 and t >= 2 * TC:
                    mix_basis(t // TC - 2)
            mix_basis(NC - 2)
            mix_basis(NC - 1)

        @block.scalar
        def _(act):
            for name, dst in ((b_ih, bi4), (b_hh, bh4)):
                act.dma_start(dst[:, :, :], name.rearrange("(g j c) -> j g c", g=3, j=NJ)).then_inc(ld_rec, 16)
            for j in range(NJ):
                act.dma_start(h0[Q * j:Q * (j + 1), :], cond[:, FJ * j:FJ * (j + 1)]).then_inc(ld_x0, 16)
            act.dma_start(amp[:, :, :], amplitudes).then_inc(ld_mix, 16)
            act.dma_start(scale_e[:, :], expert_scale.rearrange("(e o) -> e o", o=1)).then_inc(ld_mix, 16)
            act.wait_ge(ld_rec, 16 * (3 * NJ + 2))
            act.activation(whh[:, :, 0:D], whh[:, :, 0:D], ACT.Copy, scale=0.5).then_inc(whh_scaled, 1)

            def tanh_rz(t):
                act.wait_ge(gates_ready, t + 1)
                act.activation(trz[:, :], gates[t % 2][:, R:R + 2 * FJ], ACT.Tanh, scale=0.5).then_inc(rz_ready, 1)

            def tanh_n(t):
                act.wait_ge(pre_ready, t + 1)
                act.activation(sc_add[:, :, 0], pre[:, :], ACT.Tanh).then_inc(n_ready, 1)

            def hi_router():
                act.wait_ge(ld_router, 16 * NJ)
                act.activation(whi[:, :, ROUTER:WCOLS], wraw[:, :, ROUTER:WCOLS], ACT.Copy).then_inc(w_hi, 1)

            def hi_unit(u):
                act.wait_ge(ld_unit[u], 16 * 2 * NJ)
                cols = slice(2 * UW * u, 2 * UW * (u + 1))
                act.activation(whi[:, :, cols], wraw[:, :, cols], ACT.Copy).then_inc(w_hi, 1)

            def hi_down():
                act.wait_ge(ld_down, 32)
                act.activation(dhi_w[:, :, :], draw[:, :, :], ACT.Copy).then_inc(w_hi, 1)

            def tanh_gate(n):
                act.wait_ge(unit_ready, n + 1)
                if n >= 2:
                    act.wait_ge(p1_ready, n - 1)
                act.activation(th[:, n % 2, :], unit_bank[n % NB][:, 0:UW], ACT.Tanh, scale=0.5)\
                    .then_inc(th_ready, 1)

            def softmax_exp(p):
                act.wait_ge(topk_step, TOPK_STEPS * p + 4)
                act.activation(ex[:, :], lx[:, 0:E], ACT.Exp, bias=negmax[:, :], accum_out=exsum[:, :])\
                    .then_inc(ex_ready, 1)

            def copy_emT(p):
                act.wait_ge(emT_turned, p + 1)
                act.activation(emT[:, :], route[:, EMT], ACT.Copy).then_inc(emT_ready, 1)

            def hi_turned(p):
                act.wait_ge(turned_ready, p + 1)
                if p >= 1:
                    act.wait_ge(down_ready, p)
                act.activation(dhi[:, :, :], turned[:, 0:3 * P].rearrange("p (a b) -> p a b", a=3), ACT.Copy)\
                    .then_inc(dhi_ready, 1)

            def slot(c, k):
                p = c - 1
                if c == 0:
                    if k == 1:
                        hi_router()
                        hi_unit(0)
                    if k == 2:
                        hi_unit(1)
                        hi_unit(2)
                    if k == 3:
                        hi_unit(3)
                        hi_unit(4)
                    return
                if k == 0:
                    if p >= 1:
                        tanh_gate(NU * p - 1)
                    if p < NC:
                        softmax_exp(p)
                    if p == 0:
                        hi_down()
                if k == 1 and p < NC:
                    tanh_gate(NU * p)
                if k == 2:
                    if p < NC:
                        tanh_gate(NU * p + 1)
                        copy_emT(p)
                    if p >= 1:
                        hi_turned(p - 1)
                if k == 3 and p < NC:
                    tanh_gate(NU * p + 2)
                    tanh_gate(NU * p + 3)

            for c in range(NC):
                for k in range(TC):
                    t = TC * c + k
                    tanh_rz(t)
                    tanh_n(t)
                    slot(c, k)
            for k in range(TC):
                slot(NC, k)
            slot(NC + 1, 0)
            slot(NC + 1, 2)

        @block.tensor
        def _(pe):
            def x_part(t):
                g = gates[t % 2]
                for j in range(NJ):
                    pe.matmul(g[Q * j:Q * (j + 1), 0:4 * FJ], pick[0:2 * Q + NJ, j, :], bias3[0:2 * Q + NJ, :],
                              start=True, stop=False, skip_group_check=True)
                for s in range(KB):
                    for j in range(NJ):
                        pe.matmul(g[Q * j:Q * (j + 1), R:4 * FJ], xT[:, t, B * s:B * (s + 1)],
                                  wih[:, s, :].rearrange("p (g j c) -> p j g c", g=3, j=NJ)[:, j],
                                  start=False, stop=False, skip_group_check=True)

            def h_part(t):
                pe.wait_ge(hT_ready, t + 1)
                g = gates[t % 2]
                for s in range(KB):
                    for j in range(NJ):
                        st = hT0[:, B * s:B * (s + 1)] if t == 0 else hT[:, (t - 1) // TC % 2, s, (t - 1) % TC, :]
                        last = pe.matmul(g[Q * j:Q * (j + 1), HN:HN + 3 * FJ], st,
                                         whh[:, s, :].rearrange("p (g j c) -> p j g c", g=3, j=NJ)[:, j],
                                         start=False, stop=(s == KB - 1), skip_group_check=True)
                last.then_inc(gates_ready, 1)

            def three(dst, p, cols, blocks):
                for s in blocks:
                    for n, (st, w) in enumerate(((hThi, whi), (hThi, wlo), (hTlo, whi))):
                        last = pe.matmul(dst, st[:, p % 2, s, :, :].rearrange("p t b -> p (t b)"), w[:, s, cols],
                                         start=(s == 0 and n == 0), stop=(s == KB - 1 and n == 2))
                return last

            def logits(p):
                pe.wait_ge(hTlo_ready, TC * (p + 1))
                if p == 0:
                    pe.wait_ge(w_lo, 1)
                else:
                    pe.wait_ge(coef_ready, p)
                three(route[:, LOGITS], p, slice(ROUTER, WCOLS), range(KB)).then_inc(logits_ready, 1)

            def unit(n, blocks):
                p, u = n // NU, n % NU
                if p == 0:
                    pe.wait_ge(w_lo, u + 2)
                if n >= NB and 0 in blocks:
                    pe.wait_ge(q_ready, n - NB + 1)
                last = three(unit_bank[n % NB][:, :], p, slice(2 * UW * u, 2 * UW * (u + 1)), blocks)
                if KB - 1 in blocks:
                    last.then_inc(unit_ready, 1)

            def turn_em(p):
                pe.wait_ge(topk_step, TOPK_STEPS * p + 6)
                pe.transpose(route[:, EMT], em[:, :], ident[:, :]).then_inc(emT_turned, 1)

            def coefficients(p):
                if p == 0:
                    pe.wait_ge(mix_step, 6)
                pe.wait_ge(emT_ready, p + 1)
                pe.matmul(route[:, COEF], emT[:, :], mix[:, :], start=True, stop=True).then_inc(coef_psum, 1)

            def turn_hidden(p):
                pe.wait_ge(q_ready, NU * (p + 1))
                pe.wait_ge(pool_mix, 4 * (p + 1))
                pe.transpose(turned[:, 0:P], mixed[:, :], ident[:, :])
                pe.transpose(turned[:, P:2 * P], shared[:, p % 2, 0:P], ident[:, :])
                pe.transpose(turned[:, 2 * P:3 * P], shared[:, p % 2, P:2 * P], ident[:, :]).then_inc(turned_ready, 1)

            def project(p):
                if p == 0:
                    pe.wait_ge(w_lo, SPLITS)
                pe.wait_ge(dlo_ready, p + 1)
                if p >= 1:
                    pe.wait_ge(out_ready, p)
                for a in range(3):
                    for n, (st, w) in enumerate(((dhi, dhi_w), (dhi, dlo_w), (dlo, dhi_w))):
                        last = pe.matmul(down[:, 0:D], st[:, a, :], w[:, a, :],
                                         start=(a == 0 and n == 0), stop=(a == 2 and n == 2))
                last.then_inc(down_ready, 1)

            def filler(c, k):
                p = c - 1
                if p < 0:
                    return
                live = p < NC
                if k == 0 and live:
                    logits(p)
                    unit(NU * p, range(KB))
                if k == 1 and live:
                    unit(NU * p + 1, range(KB))
                    unit(NU * p + 2, [0])
                if k == 2:
                    if live:
                        turn_em(p)
                    if p >= 1:
                        turn_hidden(p - 1)
                    if live:
                        unit(NU * p + 2, [1])
                        unit(NU * p + 3, range(KB))
                        coefficients(p)
                if k == 3:
                    if p >= 1:
                        project(p - 1)
                    if live:
                        unit(NU * p + 4, range(KB))

            pe.wait_ge(const_ready, 10)
            pe.wait_ge(bias_step, 11)
            pe.wait_ge(x_turned, 1)
            x_part(0)
            pe.wait_ge(whh_scaled, 1)
            for c in range(NC):
                for k in range(TC):
                    t = TC * c + k
                    h_part(t)
                    if t + 1 < T:
                        if t + 1 == TC:
                            pe.wait_ge(x_turned, 2)
                        x_part(t + 1)
                    filler(c, k)
            for k in range(TC):
                filler(NC, k)
            filler(NC + 1, 2)
            filler(NC + 1, 3)

        @block.vector
        def _(dve):
            dve.wait_ge(ld_rec, 16 * (3 * NJ + 2))
            dve.wait_ge(const_ready, 6)
            dve.tensor_scalar(bsum[:, 0, HN:HN + FJ], bh4[:, 2, :], 0.5, None, ALU.mult).then_inc(bias_step, 1)
            dve.tensor_tensor(bsum[:, 0, R:R + 2 * FJ].rearrange("j (g c) -> j g c", g=2), bi4[:, 0:2, :], bh4[:, 0:2, :],
                              ALU.add).then_inc(bias_step, 1)
            dve.tensor_copy(bsum[:, 0, IN:IN + FJ], bi4[:, 2, :]).then_inc(bias_step, 1)
            dve.wait_ge(bias_step, 3)
            for a in range(3):
                dve.tensor_copy(bpart[:, a, :], bsum[:, a, :]).then_inc(bias_step, 1)
                dve.wait_ge(bias_step, 4 + 3 * a)
                dve.tensor_copy(bias3[Q * a:Q * a + NJ, :], bpart[:, a, :]).then_inc(bias_step, 1)
                if a < 2:
                    dve.tensor_tensor(bsum[:, a + 1, :], bsum[:, a, :], bpart[:, a, :], ALU.subtract)\
                        .then_inc(bias_step, 1)
                    dve.wait_ge(bias_step, 6 + 3 * a)

            dve.wait_ge(ld_x0, 16 * 2 * NJ)
            dve.transpose(hT0[:, :], h0[:, :]).then_inc(hT_ready, 1)
            dve.tensor_scalar(hhalf[:, :], h0[:, :], 0.5, None, ALU.mult).then_inc(hhalf_ready, 1)
            dve.transpose(xT[:, 0:TC, :].rearrange("p t f -> p (t f)"),
                          xj[:, 0:TC, :].rearrange("p t f -> p (t f)")).then_inc(x_turned, 1)

            def gru_step(t):
                c, k = t // TC, t % TC
                g = gates[t % 2]
                dve.wait_ge(rz_ready, t + 1)
                dve.scalar_tensor_tensor(out=m[:, :], in0=trz[:, 0:FJ], scalar=1.0, in1=g[:, HN:HN + FJ],
                                         op0=ALU.add, op1=ALU.mult).then_inc(m_ready, 1)
                dve.wait_ge(m_ready, t + 1)
                dve.tensor_tensor(pre[:, :], m[:, :], g[:, IN:IN + FJ], ALU.add).then_inc(pre_ready, 1)
                dve.tensor_scalar(sc_mul[:, :, 1], trz[:, FJ:2 * FJ], -0.5, 0.5, ALU.mult, ALU.add)\
                    .then_inc(blend_ready, 1)
                dve.wait_ge(hhalf_ready, t + 1)
                dve.scalar_tensor_tensor(out=sc_add[:, :, 1], in0=trz[:, FJ:2 * FJ], scalar=1.0, in1=hhalf[:, :],
                                         op0=ALU.add, op1=ALU.mult).then_inc(blend_ready, 1)
                dve.wait_ge(blend_ready, 2 * (t + 1))
                dve.wait_ge(n_ready, t + 1)
                dve.tensor_tensor_scan(sc_out[:, :, :].rearrange("p f a -> p (f a)"),
                                       sc_mul[:, :, :].rearrange("p f a -> p (f a)"),
                                       sc_add[:, :, :].rearrange("p f a -> p (f a)"),
                                       0.0, ALU.mult, ALU.add).then_inc(h_ready, 1)
                dve.wait_ge(h_ready, t + 1)
                if k == 0 and c >= 2:
                    dve.wait_ge(hTlo_ready, TC * (c - 1))
                dve.transpose(hT[:, c % 2, :, k, :], sc_out[:, :, 1]).then_inc(hT_ready, 1)
                dve.tensor_scalar(hhalf[:, :], sc_out[:, :, 1], 0.5, None, ALU.mult).then_inc(hhalf_ready, 1)

            def lo_router():
                dve.wait_ge(w_hi, 1)
                dve.tensor_tensor(wlo[:, :, ROUTER:WCOLS], wraw[:, :, ROUTER:WCOLS],
                                  whi[:, :, ROUTER:WCOLS].bitcast(F32), ALU.subtract).then_inc(w_lo, 1)

            def lo_unit(u):
                dve.wait_ge(w_hi, u + 2)
                cols = slice(2 * UW * u, 2 * UW * (u + 1))
                dve.tensor_tensor(wlo[:, :, cols], wraw[:, :, cols], whi[:, :, cols].bitcast(F32), ALU.subtract)\
                    .then_inc(w_lo, 1)

            def lo_down():
                dve.wait_ge(w_hi, SPLITS)
                dve.tensor_tensor(dlo_w[:, :, :], draw[:, :, :], dhi_w[:, :, :].bitcast(F32), ALU.subtract)\
                    .then_inc(w_lo, 1)

            def mixing_table():
                dve.wait_ge(ld_mix, 32)
                dve.tensor_tensor(amp2[:, :, :], amp[:, :, :], amp[:, :, :], ALU.mult).then_inc(mix_step, 1)
                dve.wait_ge(mix_step, 1)
                dve.tensor_tensor(pk[:, :], amp2[:, :, 0], amp2[:, :, 1], ALU.add).then_inc(mix_step, 1)
                dve.wait_ge(mix_step, 2)
                dve.tensor_reduce(psum_k[:, :], pk[:, :], mybir.AxisListType.X, ALU.add).then_inc(mix_step, 1)
                dve.wait_ge(mix_step, 3)
                dve.tensor_scalar(prec[:, :], psum_k[:, :], EPS, None, ALU.add).then_inc(mix_step, 1)
                dve.wait_ge(mix_step, 4)
                dve.reciprocal(prec[:, :], prec[:, :]).then_inc(mix_step, 1)
                dve.wait_ge(mix_step, 5)
                dve.tensor_scalar(mix[:, :], pk[:, :], prec[:, :], scale_e[:, :], ALU.mult, ALU.mult)\
                    .then_inc(mix_step, 1)

            def gated(n):
                p, u = n // NU, n % NU
                ub = unit_bank[n % NB]
                dve.wait_ge(th_ready, n + 1)
                if n >= 2:
                    dve.wait_ge(q_ready, n - 1)
                dve.scalar_tensor_tensor(out=p1[:, n % 2, :], in0=th[:, n % 2, :], scalar=1.0, in1=ub[:, 0:UW],
                                         op0=ALU.add, op1=ALU.mult).then_inc(p1_ready, 1)
                dve.wait_ge(p1_ready, n + 1)
                if u == 0 and p >= 2:
                    dve.wait_ge(pool_mix, 4 * (p - 2) + 1)
                dst = q[:, p % 2, UW * u:UW * (u + 1)] if u < NU - 1 else shared[:, p % 2, :]
                dve.scalar_tensor_tensor(out=dst, in0=p1[:, n % 2, :], scalar=0.5, in1=ub[:, UW:2 * UW],
                                         op0=ALU.mult, op1=ALU.mult).then_inc(q_ready, 1)

            def topk_mark(p):
                s = TOPK_STEPS * p
                dve.wait_ge(logits_ready, p + 1)
                dve.tensor_copy(lx[:, 0:E], route[:, LOGITS]).then_inc(topk_step, 1)
                dve.wait_ge(topk_step, s + 1)
                dve.max(v8[:, :], lx[:, 0:E]).then_inc(topk_step, 1)
                dve.wait_ge(topk_step, s + 2)
                dve.tensor_copy(keys[:, 0:TOPK], v8[:, 0:TOPK]).then_inc(topk_step, 1)
                dve.tensor_scalar(negmax[:, :], v8[:, 0:1], -1.0, None, ALU.mult).then_inc(topk_step, 1)
                dve.wait_ge(topk_step, s + 3)
                dve.match_replace(out=marked[:, :], in_to_replace=keys[:, :], in_values=lx[:, :],
                                  imm_value=HIGHEST).then_inc(topk_step, 1)

            def topk_weights(p):
                s = TOPK_STEPS * p
                dve.wait_ge(topk_step, s + 5)
                dve.wait_ge(ex_ready, p + 1)
                dve.scalar_tensor_tensor(out=em[:, :], in0=marked[:, 0:E], scalar=HIGHEST, in1=ex[:, :],
                                         op0=ALU.is_equal, op1=ALU.mult, accum_out=sum4[:, :]).then_inc(topk_step, 1)
                dve.wait_ge(topk_step, s + 6)
                dve.scalar_tensor_tensor(out=den[:, :], in0=exsum[:, :], scalar=EPS, in1=sum4[:, :],
                                         op0=ALU.mult, op1=ALU.add).then_inc(topk_step, 1)
                dve.wait_ge(topk_step, s + 7)
                dve.reciprocal(rec[:, :], den[:, :]).then_inc(topk_step, 1)

            def scale_coefficients(p):
                dve.wait_ge(topk_step, TOPK_STEPS * (p + 1))
                dve.wait_ge(coef_psum, p + 1)
                dve.tensor_scalar(coef[:, p % 2, :], route[:, COEF], rec[:, :], None, ALU.mult)\
                    .then_inc(coef_ready, 1)

            def lo_turned(p):
                dve.wait_ge(dhi_ready, p + 1)
                dve.tensor_tensor(dlo[:, :, :], turned[:, 0:3 * P].rearrange("p (a b) -> p a b", a=3),
                                  dhi[:, :, :].bitcast(F32), ALU.subtract).then_inc(dlo_ready, 1)

            def residual(p):
                dve.wait_ge(down_ready, p + 1)
                if p == 0:
                    dve.wait_ge(ld_xtok, 16 * TC)
                if p >= 2:
                    dve.wait_ge(stored[p % 2], 16 * TC * (p // 2))
                dve.tensor_tensor(ot[:, p % 2, :], down[:, 0:D], xtok[:, p, :], ALU.add).then_inc(out_ready, 1)

            def slot(c, k):
                p = c - 1
                live = 0 <= p < NC
                if c == 0:
                    if k == 0:
                        dve.wait_ge(ld_x1, 16 * NJ)
                        dve.transpose(xT[:, TC:T, :].rearrange("p t f -> p (t f)"),
                                      xj[:, TC:T, :].rearrange("p t f -> p (t f)")).then_inc(x_turned, 1)
                        mixing_table()
                    if k == 1:
                        lo_router()
                        lo_unit(0)
                    if k == 2:
                        lo_unit(1)
                        lo_unit(2)
                    if k == 3:
                        lo_unit(3)
                        lo_unit(4)
                    return
                if k == 0:
                    if p >= 1:
                        gated(NU * p - 1)
                    if live:
                        topk_mark(p)
                    if p == 0:
                        lo_down()
                if k == 1 and live:
                    topk_weights(p)
                    gated(NU * p)
                if k == 2:
                    if live:
                        gated(NU * p + 1)
                        scale_coefficients(p)
                    if p >= 1:
                        lo_turned(p - 1)
                if k == 3:
                    if live:
                        gated(NU * p + 2)
                        gated(NU * p + 3)
                    if p >= 1:
                        residual(p - 1)

            for c in range(NC):
                for k in range(TC):
                    gru_step(TC * c + k)
                    slot(c, k)
            for k in range(TC):
                slot(NC, k)
            slot(NC + 1, 0)
            slot(NC + 1, 2)
            slot(NC + 1, 3)


_INS = ['x', 'cond_2048', 'L0_cond_W_ih', 'L0_cond_W_hh', 'L0_cond_b_ih', 'L0_cond_b_hh', 'L0_ffn_w_router',
        'L0_ffn_w_gate', 'L0_ffn_w_up', 'L0_ffn_w_down', 'L0_ffn_amplitudes', 'L0_ffn_expert_scale',
        'L0_ffn_shared_w_gate', 'L0_ffn_shared_w_up', 'L0_ffn_shared_w_down']
_OUT = ((B, T, D), 'float32')


def kernel(**inputs):
    import numpy as _np
    import concourse.bacc as _bacc
    from concourse import mybir as _mybir
    from concourse.bass_utils import run_bass_kernel_spmd as _run

    nc = _bacc.Bacc("TRN2", target_bir_lowering=False, num_devices=1)
    arrays, args = {}, []
    for name in _INS:
        a = _np.ascontiguousarray(inputs[name])
        arrays[f"in_{name}_dram"] = a
        args.append(nc.dram_tensor(f"in_{name}_dram", a.shape, _mybir.dt.from_np(a.dtype), kind="ExternalInput").ap())
    shape, dtype = _OUT
    out = nc.dram_tensor("out_0_dram", shape, _mybir.dt.from_np(_np.dtype(dtype)), kind="ExternalOutput").ap()
    build(nc, *args, out)
    r = _run(nc, [arrays], core_ids=[0])
    return r.results[0]["out_0_dram"]
```

```python
from contextlib import ExitStack

import concourse.bass as bass
from concourse import mybir

F32 = mybir.dt.float32
F32R = mybir.dt.float32r
BF16 = mybir.dt.bfloat16
ALU = mybir.AluOpType
ACT = mybir.ActivationFunctionType

B, T, D = 32, 32, 256
P = 128
Q = 32
NJ = P // Q
FJ = D // NJ
KB = D // P
TC = P // B
NC = T // TC
E, K, I = 128, 8, 128
TOPK, EPS = 4, 1e-8
UW = 256
NU = K * I // UW + 1
ROUTER = 2 * UW * NU
WCOLS = ROUTER + E
RING = 2
NB = 3
LOWEST, HIGHEST = -3.0e38, 3.0e38
FIRST = 2
HN, R, Z, IN = 0, FJ, 2 * FJ, 3 * FJ


def build(nc, x, cond, w_ih, w_hh, b_ih, b_hh, w_router, w_gate, w_up, w_down, amplitudes, expert_scale,
          sw_gate, sw_up, sw_down, out):
    with ExitStack() as ctx:
        def sb(name, shape, dt=F32):
            return ctx.enter_context(nc.sbuf_tensor(name, shape, dt))

        def bank(name):
            return ctx.enter_context(nc.psum_tensor(name, [P, 512], F32))

        def sem(name):
            return ctx.enter_context(nc.semaphore(name))

        whh = sb("whh", [P, KB, 3 * D])
        wih = sb("wih", [P, KB, 3 * D])
        wraw = sb("wraw", [P, KB, WCOLS])
        whi = sb("whi", [P, KB, WCOLS], F32R)
        wlo = sb("wlo", [P, KB, WCOLS], F32R)
        draw = sb("draw", [P, 3, D])
        dhi_w = sb("dhi_w", [P, 3, D], F32R)
        dlo_w = sb("dlo_w", [P, 3, D], F32R)
        bi4 = sb("bi4", [NJ, 3, FJ])
        bh4 = sb("bh4", [NJ, 3, FJ])
        bsum = sb("bsum", [NJ, 3, 4 * FJ])
        bpart = sb("bpart", [NJ, 3, 4 * FJ], BF16)
        bias3 = sb("bias3", [P, 4 * FJ], BF16)
        pick = sb("pick", [P, NJ, Q], BF16)
        pick_tok = sb("pick_tok", [P, NJ, P], BF16)
        ident = sb("ident", [P, P])
        ident_r = sb("ident_r", [P, P], F32R)
        wih_hi = sb("wih_hi", [P, KB, 3 * D], F32R)
        wih_lo = sb("wih_lo", [P, KB, 3 * D], F32R)
        amp = sb("amp", [P, K, 2])
        amp2 = sb("amp2", [P, K, 2])
        pk = sb("pk", [P, K])
        psum_k = sb("psum_k", [P, 1])
        prec = sb("prec", [P, 1])
        scale_e = sb("scale_e", [P, 1])
        mix = sb("mix", [P, K])
        xj = sb("xj", [P, T, FJ])
        xT = sb("xT", [P, T, FJ])
        xtok = sb("xtok", [P, NC, D])
        h0 = sb("h0", [P, FJ])
        x_hi = sb("x_hi", [P, 2, KB, B, TC], F32R)
        x_lo = sb("x_lo", [P, 2, KB, B, TC], F32R)
        gi_raw = sb("gi_raw", [P, NJ, 4 * FJ])
        gi_halves = sb("gi_halves", [P, 2, NJ, 2, 4 * FJ], F32R)
        gi = sb("gi", [P, RING, TC, 2, 4 * FJ], F32R)
        hT0 = sb("hT0", [P, FJ])
        hT = sb("hT", [P, 2, KB, TC, B])
        hThi = sb("hThi", [P, 2, KB, TC, B], F32R)
        hTlo = sb("hTlo", [P, 2, KB, TC, B], F32R)
        hhalf = sb("hhalf", [P, FJ])
        trz = sb("trz", [P, 2 * FJ])
        m = sb("m", [P, FJ])
        pre = sb("pre", [P, FJ])
        sc_mul = sb("sc_mul", [P, FJ, 2])
        sc_add = sb("sc_add", [P, FJ, 2])
        sc_out = sb("sc_out", [P, FJ, 2])
        th = sb("th", [P, 2, UW])
        p1 = sb("p1", [P, 2, UW])
        q = sb("q", [P, 2, K * I])
        shared = sb("shared", [P, 2, 2 * I])
        lx = sb("lx", [P, E + TOPK])
        v8 = sb("v8", [P, 8])
        keys = sb("keys", [P, 8])
        negmax = sb("negmax", [P, 1])
        ex = sb("ex", [P, E])
        exsum = sb("exsum", [P, 1])
        marked = sb("marked", [P, E + TOPK])
        em = sb("em", [P, E])
        sum4 = sb("sum4", [P, 1])
        den = sb("den", [P, 1])
        rec = sb("rec", [P, 1])
        emT = sb("emT", [P, P])
        coef = sb("coef", [P, 2, K])
        qc = sb("qc", [P, K * I])
        half = sb("half", [P, 4 * I])
        quarter = sb("quarter", [P, 2 * I])
        mixed = sb("mixed", [P, I])
        dhi = sb("dhi", [P, 3, P], F32R)
        dlo = sb("dlo", [P, 3, P], F32R)
        ot = sb("ot", [P, 2, D])

        gates = [bank("gates0"), bank("gates1")]
        unit_bank = [bank(f"unit{n}") for n in range(NB)]
        route = bank("route")
        turned = bank("turned")
        down = bank("down")
        gi_bank = [turned, down]
        LOGITS, EMT, COEF = slice(0, E), slice(E, 2 * E), slice(2 * E, 2 * E + K)

        ld_bias = sem("ld_bias")
        ld_wih = sem("ld_wih")
        ld_whh = sem("ld_whh")
        ld_h0 = sem("ld_h0")
        ld_x0 = sem("ld_x0")
        ld_x1 = sem("ld_x1")
        ld_x2 = sem("ld_x2")
        ld_xtok = sem("ld_xtok")
        ld_mix = sem("ld_mix")
        ld_unit = [sem(f"ld_unit{u}") for u in range(NU)]
        ld_router = sem("ld_router")
        ld_down = sem("ld_down")
        const_ready = sem("const_ready")
        ident_ready = sem("ident_ready")
        wih_split = sem("wih_split")
        xhi_ready = sem("xhi_ready")
        xlo_ready = sem("xlo_ready")
        gi_psum = sem("gi_psum")
        gi_copied = sem("gi_copied")
        gi_hi = sem("gi_hi")
        gi_lo = sem("gi_lo")
        gi_loaded = [sem(f"gi_loaded{n}") for n in range(RING)]
        omz_ready = sem("omz_ready")
        lx_ready = sem("lx_ready")
        tail_mix = sem("tail_mix")
        bias_step = sem("bias_step")
        mix_step = sem("mix_step")
        x_turned = sem("x_turned")
        w_hi = sem("w_hi")
        w_lo = sem("w_lo")
        gates_ready = sem("gates_ready")
        rz_ready = sem("rz_ready")
        m_ready = sem("m_ready")
        pre_ready = sem("pre_ready")
        n_ready = sem("n_ready")
        blend_ready = sem("blend_ready")
        h_ready = sem("h_ready")
        hT_ready = sem("hT_ready")
        hhalf_ready = sem("hhalf_ready")
        hThi_ready = sem("hThi_ready")
        hTlo_ready = sem("hTlo_ready")
        logits_ready = sem("logits_ready")
        unit_ready = sem("unit_ready")
        th_ready = sem("th_ready")
        p1_ready = sem("p1_ready")
        q_ready = sem("q_ready")
        topk_step = sem("topk_step")
        ex_ready = sem("ex_ready")
        emT_turned = sem("emT_turned")
        emT_ready = sem("emT_ready")
        coef_psum = sem("coef_psum")
        coef_ready = sem("coef_ready")
        pool_mix = sem("pool_mix")
        turned_ready = sem("turned_ready")
        dhi_ready = sem("dhi_ready")
        dlo_ready = sem("dlo_ready")
        down_ready = sem("down_ready")
        out_ready = sem("out_ready")
        stored = [sem("stored0"), sem("stored1")]

        TOPK_STEPS = 7
        SPLITS = NU + 2
        block = ctx.enter_context(nc.Block())

        def rows(w, s):
            return w.rearrange("(j s c) n -> s j c n", j=NJ, s=KB)[s]

        def gi_slot(n, a):
            early = {(FIRST, 0): (0, 1), (FIRST, 1): (0, 2), (FIRST + 1, 0): (0, 3), (FIRST + 1, 1): (1, 0)}
            return early.get((n, a), (n - 2, a))

        def gi_index(n, a):
            return 2 * (n - FIRST) + a

        def gi_due(c, k):
            return [(n, a) for n in range(FIRST, NC) for a in range(2) if gi_slot(n, a) == (c, k)]

        def x_due(c, k):
            early = {FIRST: (0, 0), FIRST + 1: (0, 2)}
            return [n for n in range(FIRST, NC) if early.get(n, (n - 3, 3)) == (c, k)]

        def after(c, k):
            return (c, k - 1) if k else (c - 1, TC - 1)

        def unit_order(p):
            return list(range(NU)) if p < NC - 1 else [NU - 1] + list(range(NU - 1))

        @block.sync
        def _(sp):
            for j in range(NJ):
                sp.dma_start(xj[Q * j:Q * (j + 1), 0:2 * TC, :], x[:, 0:2 * TC, FJ * j:FJ * (j + 1)])\
                    .then_inc(ld_x0, 16)
            for s in range(KB):
                sp.dma_start(wih[:, s, :], rows(w_ih, s)).then_inc(ld_wih, 16)
            for s in range(KB):
                sp.dma_start(whh[:, s, 0:D], rows(w_hh, s)[:, :, 2 * D:3 * D]).then_inc(ld_whh, 16)
                sp.dma_start(whh[:, s, D:3 * D], rows(w_hh, s)[:, :, 0:2 * D]).then_inc(ld_whh, 16)
            for j in range(NJ):
                sp.dma_start(xj[Q * j:Q * (j + 1), 2 * TC:4 * TC, :], x[:, 2 * TC:4 * TC, FJ * j:FJ * (j + 1)])\
                    .then_inc(ld_x1, 16)
            for s in range(KB):
                sp.dma_start(wraw[:, s, ROUTER:WCOLS], rows(w_router, s)).then_inc(ld_router, 16)
            for u in range(NU):
                g, up, at = (w_gate, w_up, UW * u) if u < NU - 1 else (sw_gate, sw_up, 0)
                c0 = 2 * UW * u
                for s in range(KB):
                    sp.dma_start(wraw[:, s, c0:c0 + UW], rows(g, s)[:, :, at:at + UW]).then_inc(ld_unit[u], 16)
                    sp.dma_start(wraw[:, s, c0 + UW:c0 + 2 * UW], rows(up, s)[:, :, at:at + UW])\
                        .then_inc(ld_unit[u], 16)
            for j in range(NJ):
                sp.dma_start(xj[Q * j:Q * (j + 1), 4 * TC:T, :], x[:, 4 * TC:T, FJ * j:FJ * (j + 1)])\
                    .then_inc(ld_x2, 16)
            sp.dma_start(draw[:, 0, :], w_down).then_inc(ld_down, 16)
            sp.dma_start(draw[:, 1:3, :], sw_down.rearrange("(s p) n -> p s n", p=P)).then_inc(ld_down, 16)
            for t in range(TC):
                sp.dma_start(xtok[Q * t:Q * (t + 1), :, :],
                             x.rearrange("b (c t) d -> t b c d", t=TC)[t]).then_inc(ld_xtok, 16)

            def relayout(n):
                sp.wait_ge(gi_lo, gi_index(n, 1) + 1)
                if n >= FIRST + RING:
                    sp.wait_ge(gates_ready, TC * (n - RING + 1))
                for j in range(NJ):
                    sp.dma_start(gi[Q * j:Q * (j + 1), n % RING].bitcast(F32)
                                 .rearrange("b t a n -> b t (a n)"),
                                 gi_halves[:, n % 2, j].bitcast(F32).rearrange("p a n -> p (a n)"))\
                        .then_inc(gi_loaded[n % RING], 16)

            def store(p):
                sp.wait_ge(out_ready, p + 1)
                for t in range(TC):
                    sp.dma_start(out[:, TC * p + t, :], ot[Q * t:Q * (t + 1), p % 2, :])\
                        .then_inc(stored[p % 2], 16)

            relayout(FIRST)
            relayout(FIRST + 1)
            for p in range(NC):
                if FIRST + 2 + p < NC:
                    relayout(FIRST + 2 + p)
                store(p)
            for parity in range(2):
                sp.wait_ge(stored[parity], 16 * TC * (NC // 2))

        @block.gpsimd
        def _(pool):
            pool.memset(pick[:, :, :], 0.0).then_inc(const_ready, 1)
            pool.memset(bias3[:, :], 0.0).then_inc(const_ready, 1)
            pool.memset(ident[:, :], 0.0).then_inc(const_ready, 1)
            pool.memset(sc_mul[:, :, :], 0.0).then_inc(const_ready, 1)
            pool.memset(lx[:, E:E + TOPK], LOWEST).then_inc(const_ready, 1)
            pool.memset(keys[:, TOPK:8], LOWEST).then_inc(const_ready, 1)
            pool.memset(pick_tok[:, :, :], 0.0).then_inc(const_ready, 1)
            pool.wait_ge(const_ready, 7)
            for a in range(3):
                for which, width in ((pick, Q), (pick_tok, P)):
                    pool.affine_select(out=which[:, :, :], in_=which[:, :, :], compare_op=ALU.not_equal, fill=1.0,
                                       base=-Q * a, pattern=[[-1, NJ], [0, width]], channel_multiplier=1)\
                        .then_inc(const_ready, 1)
                pool.wait_ge(const_ready, 9 + 2 * a)
            pool.affine_select(out=ident[:, :], in_=ident[:, :], compare_op=ALU.not_equal, fill=1.0,
                               base=0, pattern=[[-1, P]], channel_multiplier=1).then_inc(const_ready, 1)

            def halves(t):
                c, k = t // TC, t % TC
                pool.wait_ge(hT_ready, t + 2)
                if k == 0 and c >= 2:
                    pool.wait_ge(unit_ready, NU * (c - 1))
                pool.tensor_copy(hThi[:, c % 2, :, k, :], hT[:, c % 2, :, k, :]).then_inc(hThi_ready, 1)
                pool.wait_ge(hThi_ready, t + 1)
                pool.tensor_tensor(hTlo[:, c % 2, :, k, :], hT[:, c % 2, :, k, :],
                                   hThi[:, c % 2, :, k, :].bitcast(F32), ALU.subtract).then_inc(hTlo_ready, 1)

            def mix_basis(p):
                pool.wait_ge(coef_ready, p + 1)
                pool.wait_ge(q_ready, NU * p + NU - 1)
                pool.tensor_tensor(qc[:, :].rearrange("p (k i) -> p k i", k=K),
                                   q[:, p % 2, :].rearrange("p (k i) -> p k i", k=K),
                                   coef[:, p % 2, :].rearrange("p (k o) -> p k o", o=1).to_broadcast([P, K, I]),
                                   ALU.mult).then_inc(pool_mix, 1)
                pool.wait_ge(pool_mix, 4 * p + 1)
                pool.tensor_tensor(half[:, :], qc[:, 0:4 * I], qc[:, 4 * I:8 * I], ALU.add).then_inc(pool_mix, 1)
                pool.wait_ge(pool_mix, 4 * p + 2)
                pool.tensor_tensor(quarter[:, :], half[:, 0:2 * I], half[:, 2 * I:4 * I], ALU.add)\
                    .then_inc(pool_mix, 1)
                pool.wait_ge(pool_mix, 4 * p + 3)
                if p >= 1:
                    pool.wait_ge(turned_ready, p)
                pool.tensor_tensor(mixed[:, :], quarter[:, 0:I], quarter[:, I:2 * I], ALU.add)\
                    .then_inc(pool_mix, 1)

            def lo_x(n):
                pool.wait_ge(xhi_ready, n - FIRST + 1)
                pool.tensor_tensor(x_lo[:, n % 2].rearrange("p s b t -> p t s b"),
                                   xT[:, TC * n:TC * (n + 1), :].rearrange("p t (s b) -> p t s b", s=KB),
                                   x_hi[:, n % 2].bitcast(F32).rearrange("p s b t -> p t s b"),
                                   ALU.subtract).then_inc(xlo_ready, 1)

            def lo_gi(n, a):
                pool.wait_ge(gi_hi, gi_index(n, a) + 1)
                pool.tensor_tensor(gi_halves[:, n % 2, 2 * a:2 * a + 2, 1, :], gi_raw[:, 2 * a:2 * a + 2, :],
                                   gi_halves[:, n % 2, 2 * a:2 * a + 2, 0, :].bitcast(F32),
                                   ALU.subtract).then_inc(gi_lo, 1)

            pool.wait_ge(wih_split, 1)
            pool.tensor_tensor(wih_lo[:, 1, :], wih[:, 1, :], wih_hi[:, 1, :].bitcast(F32), ALU.subtract)\
                .then_inc(wih_split, 1)
            for c in range(NC):
                for k in range(TC):
                    halves(TC * c + k)
                    for n, a in gi_due(*after(c, k)):
                        lo_gi(n, a)
                    for n in x_due(c, k):
                        lo_x(n)
                    if k == 0 and c >= 2:
                        mix_basis(c - 2)
            mix_basis(NC - 2)

        @block.scalar
        def _(act):
            for name, dst in ((b_ih, bi4), (b_hh, bh4)):
                act.dma_start(dst[:, :, :], name.rearrange("(g j c) -> j g c", g=3, j=NJ)).then_inc(ld_bias, 16)
            act.dma_start(h0[:, :], cond.rearrange("b (j c) -> j b c", j=NJ)).then_inc(ld_h0, 16)
            act.wait_ge(const_ready, 14)
            act.activation(ident_r[:, :], ident[:, :], ACT.Copy).then_inc(ident_ready, 1)
            act.wait_ge(ld_wih, 16 * KB)
            act.activation(wih_hi[:, :, :], wih[:, :, :], ACT.Copy).then_inc(wih_split, 1)

            def hi_x(n):
                act.wait_ge(x_turned, max(2, n - 1))
                if n >= FIRST + 2:
                    act.wait_ge(gi_psum, gi_index(n - 2, 1) + 1)
                act.activation(x_hi[:, n % 2].rearrange("p s b t -> p t s b"),
                               xT[:, TC * n:TC * (n + 1), :].rearrange("p t (s b) -> p t s b", s=KB),
                               ACT.Copy).then_inc(xhi_ready, 1)

            act.dma_start(amp[:, :, :], amplitudes).then_inc(ld_mix, 16)
            act.dma_start(scale_e[:, :], expert_scale.rearrange("(e o) -> e o", o=1)).then_inc(ld_mix, 16)

            def evacuate_gi(n, a):
                i = gi_index(n, a)
                act.wait_ge(gi_psum, i + 1)
                if i >= 2:
                    act.wait_ge(gi_lo, i - 1)
                act.activation(gi_raw[:, 2 * a:2 * a + 2, :],
                               gi_bank[a][:, :].rearrange("p (j n) -> p j n", j=2), ACT.Copy).then_inc(gi_copied, 1)
                act.wait_ge(gi_copied, i + 1)
                if n >= FIRST + 2 and a == 0:
                    act.wait_ge(gi_loaded[n % RING], 16 * NJ * ((n - FIRST) // RING))
                act.activation(gi_halves[:, n % 2, 2 * a:2 * a + 2, 0, :], gi_raw[:, 2 * a:2 * a + 2, :],
                               ACT.Copy).then_inc(gi_hi, 1)

            def tanh_rz(t):
                act.wait_ge(gates_ready, t + 1)
                act.activation(trz[:, :], gates[t % 2][:, R:R + 2 * FJ], ACT.Tanh, scale=0.5).then_inc(rz_ready, 1)
                act.wait_ge(rz_ready, t + 1)
                act.activation(sc_mul[:, :, 1], trz[:, FJ:2 * FJ], ACT.Copy, bias=0.5, scale=-0.5)\
                    .then_inc(omz_ready, 1)

            def tanh_n(t):
                act.wait_ge(pre_ready, t + 1)
                act.activation(sc_add[:, :, 0], pre[:, :], ACT.Tanh).then_inc(n_ready, 1)

            def hi_router():
                act.wait_ge(ld_router, 16 * KB)
                act.activation(whi[:, :, ROUTER:WCOLS], wraw[:, :, ROUTER:WCOLS], ACT.Copy).then_inc(w_hi, 1)

            def hi_unit(u):
                act.wait_ge(ld_unit[u], 16 * 2 * KB)
                cols = slice(2 * UW * u, 2 * UW * (u + 1))
                act.activation(whi[:, :, cols], wraw[:, :, cols], ACT.Copy).then_inc(w_hi, 1)

            def hi_down():
                act.wait_ge(ld_down, 32)
                act.activation(dhi_w[:, :, :], draw[:, :, :], ACT.Copy).then_inc(w_hi, 1)

            def tanh_gate(n):
                act.wait_ge(unit_ready, n + 1)
                if n >= 2:
                    act.wait_ge(p1_ready, n - 1)
                act.activation(th[:, n % 2, :], unit_bank[n % NB][:, 0:UW], ACT.Tanh, scale=0.5)\
                    .then_inc(th_ready, 1)

            def copy_logits(p):
                act.wait_ge(logits_ready, p + 1)
                act.activation(lx[:, 0:E], route[:, LOGITS], ACT.Copy).then_inc(lx_ready, 1)

            def softmax_exp(p):
                act.wait_ge(topk_step, TOPK_STEPS * p + 3)
                act.activation(ex[:, :], lx[:, 0:E], ACT.Exp, bias=negmax[:, :], accum_out=exsum[:, :])\
                    .then_inc(ex_ready, 1)

            def copy_emT(p):
                act.wait_ge(emT_turned, p + 1)
                act.activation(emT[:, :], route[:, EMT], ACT.Copy).then_inc(emT_ready, 1)

            def hi_turned(p):
                act.wait_ge(turned_ready, p + 1)
                if p >= 1:
                    act.wait_ge(down_ready, p)
                act.activation(dhi[:, :, :], turned[:, 0:3 * P].rearrange("p (a b) -> p a b", a=3), ACT.Copy)\
                    .then_inc(dhi_ready, 1)

            def slot(c, k):
                p = c - 1
                if c == 0:
                    if k == 1:
                        hi_router()
                    if k == 2:
                        hi_unit(0)
                    if k == 3:
                        hi_unit(1)
                elif k == 0:
                    copy_logits(p)
                    if p >= 1:
                        tanh_gate(NU * p - 1)
                    softmax_exp(p)
                elif k == 1:
                    tanh_gate(NU * p)
                elif k == 2:
                    tanh_gate(NU * p + 1)
                    copy_emT(p)
                    if p >= 1:
                        hi_turned(p - 1)
                elif k == 3:
                    tanh_gate(NU * p + 2)
                    tanh_gate(NU * p + 3)
                if c == 1:
                    if k < TC - 1:
                        hi_unit(2 + k)
                    else:
                        hi_down()
                for n, a in gi_due(*after(c, k)):
                    evacuate_gi(n, a)
                for n in x_due(c, k):
                    hi_x(n)

            for c in range(NC):
                for k in range(TC):
                    t = TC * c + k
                    tanh_rz(t)
                    tanh_n(t)
                    slot(c, k)
            p = NC - 1
            copy_logits(p)
            tanh_gate(NU * p - 1)
            softmax_exp(p)
            tanh_gate(NU * p)
            tanh_gate(NU * p + 1)
            copy_emT(p)
            hi_turned(p - 1)
            for u in range(2, NU):
                tanh_gate(NU * p + u)
            hi_turned(p)

        @block.tensor
        def _(pe):
            def x_part(t):
                g = gates[t % 2]
                for j in range(NJ):
                    pe.matmul(g[Q * j:Q * (j + 1), 0:4 * FJ], pick[0:2 * Q + NJ, j, :], bias3[0:2 * Q + NJ, :],
                              start=True, stop=False, skip_group_check=True)
                for s in range(KB):
                    for j in range(NJ):
                        pe.matmul(g[Q * j:Q * (j + 1), R:4 * FJ], xT[:, t, B * s:B * (s + 1)],
                                  wih[:, s, :].rearrange("p (g j c) -> p j g c", g=3, j=NJ)[:, j],
                                  start=False, stop=False, skip_group_check=True)

            def gi_part(n, a):
                dst = gi_bank[a]
                i = gi_index(n, a)
                if i >= 2:
                    pe.wait_ge(gi_copied, i - 1)
                if i == 0:
                    pe.wait_ge(wih_split, 3)
                if a == 0:
                    pe.wait_ge(xlo_ready, n - FIRST + 1)
                c = gi_slot(n, a)[0]
                if c >= 3:
                    pe.wait_ge(out_ready if a else dlo_ready, c - 2)
                for j in range(2):
                    pe.matmul(dst[:, 4 * FJ * j:4 * FJ * (j + 1)], pick_tok[0:2 * Q + NJ, 2 * a + j, :],
                              bias3[0:2 * Q + NJ, :], start=(j == 0), stop=False, skip_group_check=True)
                for s in range(KB):
                    for st, w in ((x_hi, wih_hi), (x_hi, wih_lo), (x_lo, wih_hi)):
                        last = pe.matmul(dst[:, :].rearrange("p (j n) -> p j n", j=2)[:, :, R:4 * FJ],
                                         st[:, n % 2, s, :, :].rearrange("p b t -> p (b t)"),
                                         w[:, s, :].rearrange("p (g j c) -> p j g c", g=3, j=NJ)[:, 2 * a:2 * a + 2],
                                         start=False, stop=False, skip_group_check=True)
                last.then_inc(gi_psum, 1)

            def inject(t):
                n = t // TC
                if t % TC == 0:
                    pe.wait_ge(gi_loaded[n % RING], 16 * NJ * ((n - FIRST) // RING + 1))
                for a in range(2):
                    pe.matmul(gates[t % 2][:, 0:4 * FJ], ident_r[:, :], gi[:, n % RING, t % TC, a, :],
                              start=(a == 0), stop=False, skip_group_check=True)

            def h_part(t):
                pe.wait_ge(hT_ready, t + 1)
                g = gates[t % 2]
                for s in range(KB):
                    for j in range(NJ):
                        st = hT0[:, B * s:B * (s + 1)] if t == 0 else hT[:, (t - 1) // TC % 2, s, (t - 1) % TC, :]
                        last = pe.matmul(g[Q * j:Q * (j + 1), HN:HN + 3 * FJ], st,
                                         whh[:, s, :].rearrange("p (g j c) -> p j g c", g=3, j=NJ)[:, j],
                                         start=False, stop=(s == KB - 1), skip_group_check=True)
                last.then_inc(gates_ready, 1)

            def three(dst, p, cols, blocks):
                for s in blocks:
                    for n, (st, w) in enumerate(((hThi, whi), (hThi, wlo), (hTlo, whi))):
                        last = pe.matmul(dst, st[:, p % 2, s, :, :].rearrange("p t b -> p (t b)"), w[:, s, cols],
                                         start=(s == 0 and n == 0), stop=(s == KB - 1 and n == 2))
                return last

            def logits(p):
                pe.wait_ge(hTlo_ready, TC * (p + 1))
                if p == 0:
                    pe.wait_ge(w_lo, 1)
                else:
                    pe.wait_ge(coef_ready, p)
                three(route[:, LOGITS], p, slice(ROUTER, WCOLS), range(KB)).then_inc(logits_ready, 1)

            def unit(n, blocks):
                p = n // NU
                u = unit_order(p)[n % NU]
                if p == 0:
                    pe.wait_ge(w_lo, u + 2)
                if n >= NB and 0 in blocks:
                    pe.wait_ge(q_ready, n - NB + 1)
                last = three(unit_bank[n % NB][:, :], p, slice(2 * UW * u, 2 * UW * (u + 1)), blocks)
                if KB - 1 in blocks:
                    last.then_inc(unit_ready, 1)

            def turn_em(p):
                pe.wait_ge(topk_step, TOPK_STEPS * p + 5)
                pe.transpose(route[:, EMT], em[:, :], ident[:, :]).then_inc(emT_turned, 1)

            def coefficients(p):
                if p == 0:
                    pe.wait_ge(mix_step, 6)
                pe.wait_ge(emT_ready, p + 1)
                pe.matmul(route[:, COEF], emT[:, :], mix[:, :], start=True, stop=True).then_inc(coef_psum, 1)

            def turn_hidden(p):
                pe.wait_ge(q_ready, NU * (p + 1))
                if p < NC - 1:
                    pe.wait_ge(pool_mix, 4 * (p + 1))
                else:
                    pe.wait_ge(tail_mix, K + 1)
                n = p + 4
                if n < NC:
                    pe.wait_ge(gi_copied, gi_index(n, 0) + 1)
                pe.transpose(turned[:, 0:P], mixed[:, :], ident[:, :])
                pe.transpose(turned[:, P:2 * P], shared[:, p % 2, 0:P], ident[:, :])
                pe.transpose(turned[:, 2 * P:3 * P], shared[:, p % 2, P:2 * P], ident[:, :]).then_inc(turned_ready, 1)

            def project(p):
                n = p + 4
                if n < NC:
                    pe.wait_ge(gi_copied, gi_index(n, 1) + 1)
                if p == 0:
                    pe.wait_ge(w_lo, SPLITS)
                pe.wait_ge(dlo_ready, p + 1)
                if p >= 1:
                    pe.wait_ge(out_ready, p)
                for a in range(3):
                    for n, (st, w) in enumerate(((dhi, dhi_w), (dhi, dlo_w), (dlo, dhi_w))):
                        last = pe.matmul(down[:, 0:D], st[:, a, :], w[:, a, :],
                                         start=(a == 0 and n == 0), stop=(a == 2 and n == 2))
                last.then_inc(down_ready, 1)

            def filler(c, k):
                p = c - 1
                if p >= 0:
                    if k == 0:
                        logits(p)
                        unit(NU * p, range(KB))
                    if k == 1:
                        unit(NU * p + 1, range(KB))
                        unit(NU * p + 2, [0])
                    if k == 2:
                        turn_em(p)
                        if p >= 1:
                            turn_hidden(p - 1)
                        unit(NU * p + 2, [1])
                        unit(NU * p + 3, range(KB))
                        coefficients(p)
                    if k == 3:
                        if p >= 1:
                            project(p - 1)
                        unit(NU * p + 4, range(KB))
                for n, a in gi_due(c, k):
                    gi_part(n, a)

            pe.wait_ge(const_ready, 14)
            pe.wait_ge(bias_step, 11)
            pe.wait_ge(x_turned, 1)
            pe.wait_ge(ld_wih, 16 * KB)
            x_part(0)
            pe.wait_ge(ident_ready, 1)
            pe.wait_ge(ld_whh, 16 * 2 * KB)
            for c in range(NC):
                for k in range(TC):
                    t = TC * c + k
                    h_part(t)
                    if t + 1 < TC * FIRST:
                        x_part(t + 1)
                    elif t + 1 < T:
                        inject(t + 1)
                    filler(c, k)
            p = NC - 1
            logits(p)
            unit(NU * p, range(KB))
            unit(NU * p + 1, range(KB))
            turn_em(p)
            unit(NU * p + 2, range(KB))
            coefficients(p)
            turn_hidden(p - 1)
            unit(NU * p + 3, range(KB))
            project(p - 1)
            unit(NU * p + 4, range(KB))
            turn_hidden(p)
            project(p)

        @block.vector
        def _(dve):
            dve.wait_ge(ld_bias, 32)
            dve.wait_ge(const_ready, 6)
            dve.tensor_copy(bsum[:, 0, HN:HN + FJ], bh4[:, 2, :]).then_inc(bias_step, 1)
            dve.tensor_tensor(bsum[:, 0, R:R + 2 * FJ].rearrange("j (g c) -> j g c", g=2), bi4[:, 0:2, :], bh4[:, 0:2, :],
                              ALU.add).then_inc(bias_step, 1)
            dve.tensor_copy(bsum[:, 0, IN:IN + FJ], bi4[:, 2, :]).then_inc(bias_step, 1)
            dve.wait_ge(bias_step, 3)
            for a in range(3):
                dve.tensor_copy(bpart[:, a, :], bsum[:, a, :]).then_inc(bias_step, 1)
                dve.wait_ge(bias_step, 4 + 3 * a)
                dve.tensor_copy(bias3[Q * a:Q * a + NJ, :], bpart[:, a, :]).then_inc(bias_step, 1)
                if a < 2:
                    dve.tensor_tensor(bsum[:, a + 1, :], bsum[:, a, :], bpart[:, a, :], ALU.subtract)\
                        .then_inc(bias_step, 1)
                    dve.wait_ge(bias_step, 6 + 3 * a)

            dve.wait_ge(ld_x0, 16 * NJ)
            dve.transpose(xT[:, 0:2 * TC, :].rearrange("p t f -> p (t f)"),
                          xj[:, 0:2 * TC, :].rearrange("p t f -> p (t f)")).then_inc(x_turned, 1)
            dve.wait_ge(ld_h0, 16)
            dve.transpose(hT0[:, :], h0[:, :]).then_inc(hT_ready, 1)
            dve.tensor_scalar(hhalf[:, :], h0[:, :], 0.5, None, ALU.mult).then_inc(hhalf_ready, 1)
            dve.wait_ge(wih_split, 1)
            dve.tensor_tensor(wih_lo[:, 0, :], wih[:, 0, :], wih_hi[:, 0, :].bitcast(F32), ALU.subtract)\
                .then_inc(wih_split, 1)

            def gru_step(t):
                c, k = t // TC, t % TC
                g = gates[t % 2]
                dve.wait_ge(rz_ready, t + 1)
                dve.scalar_tensor_tensor(out=m[:, :], in0=trz[:, 0:FJ], scalar=1.0, in1=g[:, HN:HN + FJ],
                                         op0=ALU.add, op1=ALU.mult).then_inc(m_ready, 1)
                dve.wait_ge(m_ready, t + 1)
                dve.scalar_tensor_tensor(out=pre[:, :], in0=m[:, :], scalar=0.5, in1=g[:, IN:IN + FJ],
                                         op0=ALU.mult, op1=ALU.add).then_inc(pre_ready, 1)
                dve.wait_ge(hhalf_ready, t + 1)
                dve.scalar_tensor_tensor(out=sc_add[:, :, 1], in0=trz[:, FJ:2 * FJ], scalar=1.0, in1=hhalf[:, :],
                                         op0=ALU.add, op1=ALU.mult).then_inc(blend_ready, 1)
                dve.wait_ge(blend_ready, t + 1)
                dve.wait_ge(n_ready, t + 1)
                dve.tensor_tensor_scan(sc_out[:, :, :].rearrange("p f a -> p (f a)"),
                                       sc_mul[:, :, :].rearrange("p f a -> p (f a)"),
                                       sc_add[:, :, :].rearrange("p f a -> p (f a)"),
                                       0.0, ALU.mult, ALU.add).then_inc(h_ready, 1)
                dve.wait_ge(h_ready, t + 1)
                if k == 0 and c >= 2:
                    dve.wait_ge(hTlo_ready, TC * (c - 1))
                dve.transpose(hT[:, c % 2, :, k, :], sc_out[:, :, 1]).then_inc(hT_ready, 1)
                dve.tensor_scalar(hhalf[:, :], sc_out[:, :, 1], 0.5, None, ALU.mult).then_inc(hhalf_ready, 1)

            def turn_x(t0, t1, loaded):
                dve.wait_ge(loaded, 16 * NJ)
                dve.transpose(xT[:, t0:t1, :].rearrange("p t f -> p (t f)"),
                              xj[:, t0:t1, :].rearrange("p t f -> p (t f)")).then_inc(x_turned, 1)

            def lo_router():
                dve.wait_ge(w_hi, 1)
                dve.tensor_tensor(wlo[:, :, ROUTER:WCOLS], wraw[:, :, ROUTER:WCOLS],
                                  whi[:, :, ROUTER:WCOLS].bitcast(F32), ALU.subtract).then_inc(w_lo, 1)

            def lo_unit(u):
                dve.wait_ge(w_hi, u + 2)
                cols = slice(2 * UW * u, 2 * UW * (u + 1))
                dve.tensor_tensor(wlo[:, :, cols], wraw[:, :, cols], whi[:, :, cols].bitcast(F32), ALU.subtract)\
                    .then_inc(w_lo, 1)

            def lo_down():
                dve.wait_ge(w_hi, SPLITS)
                dve.tensor_tensor(dlo_w[:, :, :], draw[:, :, :], dhi_w[:, :, :].bitcast(F32), ALU.subtract)\
                    .then_inc(w_lo, 1)

            def mixing_table():
                dve.wait_ge(ld_mix, 32)
                dve.tensor_tensor(amp2[:, :, :], amp[:, :, :], amp[:, :, :], ALU.mult).then_inc(mix_step, 1)
                dve.wait_ge(mix_step, 1)
                dve.tensor_tensor(pk[:, :], amp2[:, :, 0], amp2[:, :, 1], ALU.add).then_inc(mix_step, 1)
                dve.wait_ge(mix_step, 2)
                dve.tensor_reduce(psum_k[:, :], pk[:, :], mybir.AxisListType.X, ALU.add).then_inc(mix_step, 1)
                dve.wait_ge(mix_step, 3)
                dve.tensor_scalar(prec[:, :], psum_k[:, :], EPS, None, ALU.add).then_inc(mix_step, 1)
                dve.wait_ge(mix_step, 4)
                dve.reciprocal(prec[:, :], prec[:, :]).then_inc(mix_step, 1)
                dve.wait_ge(mix_step, 5)
                dve.tensor_scalar(mix[:, :], pk[:, :], prec[:, :], scale_e[:, :], ALU.mult, ALU.mult)\
                    .then_inc(mix_step, 1)

            def gated_p1(n):
                dve.wait_ge(th_ready, n + 1)
                if n >= 2:
                    dve.wait_ge(q_ready, n - 1)
                dve.scalar_tensor_tensor(out=p1[:, n % 2, :], in0=th[:, n % 2, :], scalar=1.0,
                                         in1=unit_bank[n % NB][:, 0:UW], op0=ALU.add, op1=ALU.mult)\
                    .then_inc(p1_ready, 1)

            def gated_q(n):
                p = n // NU
                u = unit_order(p)[n % NU]
                dve.wait_ge(p1_ready, n + 1)
                if n % NU == 0 and p >= 2:
                    dve.wait_ge(pool_mix, 4 * (p - 2) + 1)
                dst = q[:, p % 2, UW * u:UW * (u + 1)] if u < NU - 1 else shared[:, p % 2, :]
                dve.scalar_tensor_tensor(out=dst, in0=p1[:, n % 2, :], scalar=0.5, in1=unit_bank[n % NB][:, UW:2 * UW],
                                         op0=ALU.mult, op1=ALU.mult).then_inc(q_ready, 1)

            def topk_max(p):
                dve.wait_ge(lx_ready, p + 1)
                dve.max(v8[:, :], lx[:, 0:E]).then_inc(topk_step, 1)

            def topk_keys(p):
                dve.wait_ge(topk_step, TOPK_STEPS * p + 1)
                dve.tensor_scalar(negmax[:, :], v8[:, 0:1], -1.0, None, ALU.mult).then_inc(topk_step, 1)
                dve.tensor_copy(keys[:, 0:TOPK], v8[:, 0:TOPK]).then_inc(topk_step, 1)

            def topk_mark(p):
                dve.wait_ge(topk_step, TOPK_STEPS * p + 3)
                dve.match_replace(out=marked[:, :], in_to_replace=keys[:, :], in_values=lx[:, :],
                                  imm_value=HIGHEST).then_inc(topk_step, 1)

            def topk_em(p):
                dve.wait_ge(topk_step, TOPK_STEPS * p + 4)
                dve.wait_ge(ex_ready, p + 1)
                dve.scalar_tensor_tensor(out=em[:, :], in0=marked[:, 0:E], scalar=HIGHEST, in1=ex[:, :],
                                         op0=ALU.is_equal, op1=ALU.mult, accum_out=sum4[:, :]).then_inc(topk_step, 1)

            def topk_den(p):
                dve.wait_ge(topk_step, TOPK_STEPS * p + 5)
                dve.scalar_tensor_tensor(out=den[:, :], in0=exsum[:, :], scalar=EPS, in1=sum4[:, :],
                                         op0=ALU.mult, op1=ALU.add).then_inc(topk_step, 1)

            def topk_rec(p):
                dve.wait_ge(topk_step, TOPK_STEPS * p + 6)
                dve.reciprocal(rec[:, :], den[:, :]).then_inc(topk_step, 1)

            def mix_pair(u):
                p = NC - 1
                dve.wait_ge(q_ready, NU * p + u + 2)
                for k in (2 * u, 2 * u + 1):
                    qk, ck = q[:, p % 2, I * k:I * (k + 1)], coef[:, p % 2, k:k + 1]
                    if k == 0:
                        dve.wait_ge(coef_ready, NC)
                        dve.wait_ge(turned_ready, NC - 1)
                        dve.memset(mixed[:, :], 0.0).then_inc(tail_mix, 1)
                    dve.wait_ge(tail_mix, k + 1)
                    dve.scalar_tensor_tensor(out=mixed[:, :], in0=qk, scalar=ck, in1=mixed[:, :],
                                             op0=ALU.mult, op1=ALU.add).then_inc(tail_mix, 1)

            def scale_coefficients(p):
                dve.wait_ge(topk_step, TOPK_STEPS * (p + 1))
                dve.wait_ge(coef_psum, p + 1)
                dve.tensor_scalar(coef[:, p % 2, :], route[:, COEF], rec[:, :], None, ALU.mult)\
                    .then_inc(coef_ready, 1)

            def lo_turned(p):
                dve.wait_ge(dhi_ready, p + 1)
                dve.tensor_tensor(dlo[:, :, :], turned[:, 0:3 * P].rearrange("p (a b) -> p a b", a=3),
                                  dhi[:, :, :].bitcast(F32), ALU.subtract).then_inc(dlo_ready, 1)

            def residual(p):
                dve.wait_ge(down_ready, p + 1)
                if p == 0:
                    dve.wait_ge(ld_xtok, 16 * TC)
                if p >= 2:
                    dve.wait_ge(stored[p % 2], 16 * TC * (p // 2))
                dve.tensor_tensor(ot[:, p % 2, :], down[:, 0:D], xtok[:, p, :], ALU.add).then_inc(out_ready, 1)

            def slot(c, k):
                p = c - 1
                if c == 0:
                    if k == 0:
                        turn_x(2 * TC, 4 * TC, ld_x1)
                    if k == 1:
                        lo_router()
                        mixing_table()
                    if k == 2:
                        lo_unit(0)
                    if k == 3:
                        lo_unit(1)
                elif k == 0:
                    topk_max(p)
                    if p >= 1:
                        gated_p1(NU * p - 1)
                    topk_keys(p)
                    if p >= 1:
                        gated_q(NU * p - 1)
                    topk_mark(p)
                elif k == 1:
                    topk_em(p)
                    gated_p1(NU * p)
                    topk_den(p)
                    gated_q(NU * p)
                    topk_rec(p)
                elif k == 2:
                    gated_p1(NU * p + 1)
                    if p >= 1:
                        lo_turned(p - 1)
                    gated_q(NU * p + 1)
                    scale_coefficients(p)
                elif k == 3:
                    gated_p1(NU * p + 2)
                    gated_p1(NU * p + 3)
                    gated_q(NU * p + 2)
                    gated_q(NU * p + 3)
                    if p >= 1:
                        residual(p - 1)
                if c == 1:
                    if k < TC - 1:
                        lo_unit(2 + k)
                    else:
                        lo_down()
                for n in x_due(c, k):
                    if n >= FIRST + 2:
                        turn_x(TC * n, TC * (n + 1), ld_x2)

            for c in range(NC):
                for k in range(TC):
                    gru_step(TC * c + k)
                    slot(c, k)
            p = NC - 1
            topk_max(p)
            gated_p1(NU * p - 1)
            topk_keys(p)
            gated_q(NU * p - 1)
            topk_mark(p)
            gated_p1(NU * p)
            topk_em(p)
            gated_q(NU * p)
            topk_den(p)
            gated_p1(NU * p + 1)
            topk_rec(p)
            gated_q(NU * p + 1)
            scale_coefficients(p)
            lo_turned(p - 1)
            gated_p1(NU * p + 2)
            gated_q(NU * p + 2)
            mix_pair(0)
            mix_pair(1)
            gated_p1(NU * p + 3)
            gated_q(NU * p + 3)
            residual(p - 1)
            mix_pair(2)
            gated_p1(NU * p + 4)
            gated_q(NU * p + 4)
            mix_pair(3)
            lo_turned(p)
            residual(p)


_INS = ['x', 'cond_2048', 'L0_cond_W_ih', 'L0_cond_W_hh', 'L0_cond_b_ih', 'L0_cond_b_hh', 'L0_ffn_w_router',
        'L0_ffn_w_gate', 'L0_ffn_w_up', 'L0_ffn_w_down', 'L0_ffn_amplitudes', 'L0_ffn_expert_scale',
        'L0_ffn_shared_w_gate', 'L0_ffn_shared_w_up', 'L0_ffn_shared_w_down']
_OUT = ((B, T, D), 'float32')


def kernel(**inputs):
    import numpy as _np
    import concourse.bacc as _bacc
    from concourse import mybir as _mybir
    from concourse.bass_utils import run_bass_kernel_spmd as _run

    nc = _bacc.Bacc("TRN2", target_bir_lowering=False, num_devices=1)
    arrays, args = {}, []
    for name in _INS:
        a = _np.ascontiguousarray(inputs[name])
        arrays[f"in_{name}_dram"] = a
        args.append(nc.dram_tensor(f"in_{name}_dram", a.shape, _mybir.dt.from_np(a.dtype), kind="ExternalInput").ap())
    shape, dtype = _OUT
    out = nc.dram_tensor("out_0_dram", shape, _mybir.dt.from_np(_np.dtype(dtype)), kind="ExternalOutput").ap()
    build(nc, *args, out)
    r = _run(nc, [arrays], core_ids=[0])
    return r.results[0]["out_0_dram"]
```

```python
from contextlib import ExitStack

import concourse.bass as bass
from concourse import mybir

F32 = mybir.dt.float32
F32R = mybir.dt.float32r
BF16 = mybir.dt.bfloat16
ALU = mybir.AluOpType
ACT = mybir.ActivationFunctionType

B, T, D = 32, 32, 256
P = 128
Q = 32
NJ = P // Q
FJ = D // NJ
KB = D // P
TC = P // B
NC = T // TC
E, K, I = 128, 8, 128
TOPK, EPS = 4, 1e-8
UW = 256
NU = K * I // UW + 1
RING = 2
NB = 3
LOWEST, HIGHEST = -3.0e38, 3.0e38
FIRST = 2
HN, R, Z, IN = 0, FJ, 2 * FJ, 3 * FJ
HALF = 3 * FJ
GI = 2 * HALF + FJ
WARM = 28


def build(nc, x, cond, w_ih, w_hh, b_ih, b_hh, w_router, w_gate, w_up, w_down, amplitudes, expert_scale,
          sw_gate, sw_up, sw_down, out):
    with ExitStack() as ctx:
        def sb(name, shape, dt=F32):
            return ctx.enter_context(nc.sbuf_tensor(name, shape, dt))

        def bank(name):
            return ctx.enter_context(nc.psum_tensor(name, [P, 512], F32))

        def sem(name):
            return ctx.enter_context(nc.semaphore(name))

        whh = sb("whh", [P, KB, 3 * D])
        wih = sb("wih", [P, KB, 3 * D])
        wraw = sb("wraw", [P, KB, 2, UW * NU])
        whi = sb("whi", [P, KB, 2, UW * NU], F32R)
        wlo = sb("wlo", [P, KB, 2, UW * NU], F32R)
        rraw = sb("rraw", [P, KB, E])
        wrouter = sb("wrouter", [P, KB, 2, E], F32R)
        draw = sb("draw", [P, 3, D])
        dhi_w = sb("dhi_w", [P, 3, D], F32R)
        dlo_w = sb("dlo_w", [P, 3, D], F32R)
        bi4 = sb("bi4", [NJ, 3, FJ])
        bh4 = sb("bh4", [NJ, 3, FJ])
        bsum = sb("bsum", [NJ, 3, 4 * FJ])
        bpart = sb("bpart", [NJ, 3, 4 * FJ], BF16)
        bias3 = sb("bias3", [P, 4 * FJ], BF16)
        empty = sb("empty", [P, 2 * P], BF16)
        pick4 = sb("pick4", [NJ, NJ, Q])
        pick = sb("pick", [P, NJ, Q], BF16)
        pick_tok = sb("pick_tok", [P, NJ, P], BF16)
        ident = sb("ident", [P, P])
        ident_r = sb("ident_r", [P, P], F32R)
        wih_hi = sb("wih_hi", [P, KB, 3 * D], F32R)
        wih_lo = sb("wih_lo", [P, KB, 3 * D], F32R)
        amp = sb("amp", [P, K, 2])
        amp2 = sb("amp2", [P, K, 2])
        pk = sb("pk", [P, K])
        psum_k = sb("psum_k", [P, 1])
        prec = sb("prec", [P, 1])
        scale_e = sb("scale_e", [P, 1])
        mix = sb("mix", [P, K])
        xj = sb("xj", [P, T, FJ])
        xT = sb("xT", [P, T, FJ])
        xtok = sb("xtok", [P, NC, D])
        h0 = sb("h0", [P, FJ])
        x_hi = sb("x_hi", [P, 2, KB, B, TC], F32R)
        x_lo = sb("x_lo", [P, 2, KB, B, TC], F32R)
        bias_tok = sb("bias_tok", [P, NJ, 4 * FJ])
        gi_halves = sb("gi_halves", [P, 2, NJ, GI], F32R)
        gi = sb("gi", [P, RING, TC, GI], F32R)
        hT0 = sb("hT0", [P, FJ])
        hT = sb("hT", [P, 2, KB, TC, B])
        hThi = sb("hThi", [P, 2, KB, TC, B], F32R)
        hTlo = sb("hTlo", [P, 2, KB, TC, B], F32R)
        hhalf = sb("hhalf", [P, FJ])
        trz = sb("trz", [P, 2 * FJ])
        m = sb("m", [P, FJ])
        pre = sb("pre", [P, FJ])
        sc_mul = sb("sc_mul", [P, FJ, 2])
        sc_add = sb("sc_add", [P, FJ, 2])
        sc_out = sb("sc_out", [P, FJ, 2])
        th = sb("th", [P, 2, UW])
        p1 = sb("p1", [P, 2, UW])
        q = sb("q", [P, 2, K * I])
        shared = sb("shared", [P, 2, 2 * I])
        lx = sb("lx", [P, E + TOPK])
        v8 = sb("v8", [P, 8])
        keys = sb("keys", [P, 8])
        negmax = sb("negmax", [P, 1])
        ex = sb("ex", [P, E])
        exsum = sb("exsum", [P, 1])
        marked = sb("marked", [P, E + TOPK])
        em = sb("em", [P, E])
        sum4 = sb("sum4", [P, 1])
        den = sb("den", [P, 1])
        rec = sb("rec", [P, 1])
        emT = sb("emT", [P, P])
        coef = sb("coef", [P, 2, K])
        qc = sb("qc", [P, K * I])
        half = sb("half", [P, 4 * I])
        quarter = sb("quarter", [P, 2 * I])
        mixed = sb("mixed", [P, I])
        dhi = sb("dhi", [P, 2, 3, P], F32R)
        dlo = sb("dlo", [P, 2, 3, P], F32R)
        ot = sb("ot", [P, 2, D])

        gates = [bank("gates0"), bank("gates1")]
        unit_bank = [bank(f"unit{n}") for n in range(NB)]
        route = bank("route")
        turned = bank("turned")
        down = bank("down")
        gi_bank = [turned, down]
        LOGITS, EMT, COEF = slice(0, 2 * E), slice(2 * E, 3 * E), slice(3 * E, 3 * E + K)
        last_turned, last_down = gates[1], gates[0]
        scaled_up = qc[:, 0:2 * UW].rearrange("p (n c) -> p n c", n=2)

        ld_bias = sem("ld_bias")
        ld_wih = [sem(f"ld_wih{s}") for s in range(KB)]
        ld_whh = [sem(f"ld_whh{s}") for s in range(KB)]
        ld_h0 = sem("ld_h0")
        ld_x0 = sem("ld_x0")
        ld_x1 = sem("ld_x1")
        ld_x2 = sem("ld_x2")
        ld_xtok = sem("ld_xtok")
        ld_mix = sem("ld_mix")
        ld_routed = [sem(f"ld_routed{s}") for s in range(KB)]
        ld_shared = [sem(f"ld_shared{s}") for s in range(KB)]
        ld_router = sem("ld_router")
        ld_down = sem("ld_down")
        zeroed = sem("zeroed")
        const_ready = sem("const_ready")
        ident_ready = sem("ident_ready")
        wih_split = sem("wih_split")
        xhi_ready = sem("xhi_ready")
        xlo_ready = sem("xlo_ready")
        gi_psum = sem("gi_psum")
        bias_tok_psum = sem("bias_tok_psum")
        bias_tok_ready = sem("bias_tok_ready")
        bias_lo_ready = sem("bias_lo_ready")
        gi_biased = sem("gi_biased")
        gi_hi = sem("gi_hi")
        gi_lo = sem("gi_lo")
        gi_loaded = [sem(f"gi_loaded{n}") for n in range(RING)]
        omz_ready = sem("omz_ready")
        empty_ready = sem("empty_ready")
        lx_ready = sem("lx_ready")
        tail_mix = sem("tail_mix")
        bias_step = sem("bias_step")
        mix_step = sem("mix_step")
        x_turned = sem("x_turned")
        w_hi = sem("w_hi")
        w_lo = sem("w_lo")
        w_lo_pool = sem("w_lo_pool")
        gates_ready = sem("gates_ready")
        rz_ready = sem("rz_ready")
        m_ready = sem("m_ready")
        pre_ready = sem("pre_ready")
        n_ready = sem("n_ready")
        blend_ready = sem("blend_ready")
        h_ready = sem("h_ready")
        hT_ready = sem("hT_ready")
        hhalf_ready = sem("hhalf_ready")
        hThi_ready = sem("hThi_ready")
        hTlo_ready = sem("hTlo_ready")
        logits_ready = sem("logits_ready")
        unit_ready = sem("unit_ready")
        th_ready = sem("th_ready")
        p1_ready = sem("p1_ready")
        q_ready = sem("q_ready")
        topk_step = sem("topk_step")
        ex_ready = sem("ex_ready")
        emT_turned = sem("emT_turned")
        emT_ready = sem("emT_ready")
        coef_psum = sem("coef_psum")
        coef_ready = sem("coef_ready")
        pool_mix = sem("pool_mix")
        turned_ready = sem("turned_ready")
        up_scaled = sem("up_scaled")
        dhi_ready = sem("dhi_ready")
        dlo_ready = sem("dlo_ready")
        dlo_last = sem("dlo_last")
        down_ready = sem("down_ready")
        out_ready = sem("out_ready")
        stored = [sem("stored0"), sem("stored1")]

        TOPK_STEPS = 7
        MIX_STEPS = 5
        PIECES = [(0, 0), (1, 0), (0, 1), (1, 1), (2, 0), (2, 1), (3, 0), (3, 1), (4, 0), (4, 1)]
        LO_VECTOR = [0, 2, 3, 4, 7]
        LO_POOL = [1, 5, 6, 8, 9]
        LAST = NC - 1
        block = ctx.enter_context(nc.Block())

        def rows(w, s):
            return w.rearrange("(j s c) n -> s j c n", j=NJ, s=KB)[s]

        def gi_slot(n, a):
            early = {(FIRST, 0): (0, 1), (FIRST, 1): (0, 2), (FIRST + 1, 0): (0, 3), (FIRST + 1, 1): (1, 3)}
            return early.get((n, a), (n - 2, a))

        def gi_index(n, a):
            return 2 * (n - FIRST) + a

        def gi_due(c, k):
            return [(n, a) for n in range(FIRST, NC) for a in range(2) if gi_slot(n, a) == (c, k)]

        def x_due(c, k):
            early = {FIRST: (0, 0), FIRST + 1: (0, 1), FIRST + 2: (1, 2)}
            return [n for n in range(FIRST, NC) if early.get(n, (n - 3, 1)) == (c, k)]

        def after(c, k):
            return (c, k - 1) if k else (c - 1, TC - 1)

        def unit_order(p):
            return list(range(NU)) if p < NC - 1 else [NU - 1] + list(range(NU - 1))

        def load_x(queue, t0, t1, loaded):
            for j in range(NJ):
                queue.dma_start(xj[Q * j:Q * (j + 1), t0:t1, :], x[:, t0:t1, FJ * j:FJ * (j + 1)]).then_inc(loaded, 16)

        @block.sync
        def _(sp):
            sp.dma_start(wih[:, 0, :], rows(w_ih, 0)).then_inc(ld_wih[0], 16)
            load_x(sp, 0, TC, ld_x0)
            sp.dma_start(wih[:, 1, :], rows(w_ih, 1)).then_inc(ld_wih[1], 16)
            for s in range(KB):
                sp.dma_start(whh[:, s, 0:D], rows(w_hh, s)[:, :, 2 * D:3 * D]).then_inc(ld_whh[s], 16)
                sp.dma_start(whh[:, s, D:3 * D], rows(w_hh, s)[:, :, 0:2 * D]).then_inc(ld_whh[s], 16)
            load_x(sp, TC, 4 * TC, ld_x1)
            for s in range(KB):
                sp.dma_start(rraw[:, s, :], rows(w_router, s)).then_inc(ld_router, 16)
            for g, up, loaded, c0, c1 in ((w_gate, w_up, ld_routed, 0, K * I),
                                          (sw_gate, sw_up, ld_shared, K * I, K * I + 2 * I)):
                for s in range(KB):
                    sp.dma_start(wraw[:, s, 0, c0:c1], rows(g, s)).then_inc(loaded[s], 16)
                    sp.dma_start(wraw[:, s, 1, c0:c1], rows(up, s)).then_inc(loaded[s], 16)
            sp.dma_start(amp[:, :, :], amplitudes).then_inc(ld_mix, 16)
            sp.dma_start(scale_e[:, :], expert_scale.rearrange("(e o) -> e o", o=1)).then_inc(ld_mix, 16)
            load_x(sp, 4 * TC, T, ld_x2)
            sp.dma_start(draw[:, 0, :], w_down).then_inc(ld_down, 16)
            sp.dma_start(draw[:, 1:3, :], sw_down.rearrange("(s p) n -> p s n", p=P)).then_inc(ld_down, 16)
            for t in range(TC):
                sp.dma_start(xtok[Q * t:Q * (t + 1), :, :],
                             x.rearrange("b (c t) d -> t b c d", t=TC)[t]).then_inc(ld_xtok, 16)

            def relayout(n):
                sp.wait_ge(gi_lo, gi_index(n, 1) + 1)
                if n < FIRST + 2:
                    sp.wait_ge(bias_lo_ready, 1 + n - FIRST)
                if n >= FIRST + RING:
                    sp.wait_ge(pre_ready, TC * (n - RING + 1))
                for j in range(NJ):
                    sp.dma_start(gi[Q * j:Q * (j + 1), n % RING].bitcast(F32), gi_halves[:, n % 2, j].bitcast(F32))\
                        .then_inc(gi_loaded[n % RING], 16)

            def store(p):
                sp.wait_ge(out_ready, p + 1)
                sp.dma_start(out.rearrange("b (c t) d -> c t b d", t=TC)[p], ot[:, p % 2, :])\
                    .then_inc(stored[p % 2], 16)

            relayout(FIRST)
            relayout(FIRST + 1)
            for p in range(NC):
                if FIRST + 2 + p < NC:
                    relayout(FIRST + 2 + p)
                store(p)
            for parity in range(2):
                sp.wait_ge(stored[parity], 16 * (NC // 2))

        @block.gpsimd
        def _(pool):
            for name, dst in ((b_ih, bi4), (b_hh, bh4)):
                pool.dma_start(dst[:, :, :], name.rearrange("(g j c) -> j g c", g=3, j=NJ)).then_inc(ld_bias, 16)
            pool.dma_start(h0[:, :], cond.rearrange("b (j c) -> j b c", j=NJ)).then_inc(ld_h0, 16)
            pool.wait_ge(zeroed, 1)
            pool.affine_select(out=pick4[:, :, :], in_=pick4[:, :, :], compare_op=ALU.not_equal, fill=1.0,
                               base=0, pattern=[[-1, NJ], [0, Q]], channel_multiplier=1).then_inc(const_ready, 1)
            pool.wait_ge(zeroed, 4)
            for a in range(3):
                for which, width in ((pick, Q), (pick_tok, P)):
                    pool.affine_select(out=which[:, :, :], in_=which[:, :, :], compare_op=ALU.not_equal, fill=1.0,
                                       base=-Q * a, pattern=[[-1, NJ], [0, width]], channel_multiplier=1)\
                        .then_inc(const_ready, 1)
                pool.wait_ge(const_ready, 3 + 2 * a)
            pool.affine_select(out=ident[:, :], in_=ident[:, :], compare_op=ALU.not_equal, fill=1.0,
                               base=0, pattern=[[-1, P]], channel_multiplier=1).then_inc(const_ready, 1)

            def halves(t):
                c, k = t // TC, t % TC
                pool.wait_ge(hT_ready, t + 2)
                if k == 0 and c >= 2:
                    pool.wait_ge(unit_ready, NU * (c - 1))
                pool.tensor_copy(hThi[:, c % 2, :, k, :], hT[:, c % 2, :, k, :]).then_inc(hThi_ready, 1)
                pool.wait_ge(hThi_ready, t + 1)
                pool.tensor_tensor(hTlo[:, c % 2, :, k, :], hT[:, c % 2, :, k, :],
                                   hThi[:, c % 2, :, k, :].bitcast(F32), ALU.subtract).then_inc(hTlo_ready, 1)

            def scale_basis(p, part):
                if part == 0:
                    pool.wait_ge(coef_ready, p + 1)
                pool.wait_ge(q_ready, NU * p + 2 * (part + 1))
                ks, cols = slice(K // 2 * part, K // 2 * (part + 1)), slice(K // 2 * I * part, K // 2 * I * (part + 1))
                pool.tensor_tensor(qc[:, cols].rearrange("p (k i) -> p k i", i=I),
                                   q[:, p % 2, cols].rearrange("p (k i) -> p k i", i=I),
                                   coef[:, p % 2, ks].rearrange("p (k o) -> p k o", o=1).to_broadcast([P, K // 2, I]),
                                   ALU.mult).then_inc(pool_mix, 1)

            def add_basis(p):
                pool.wait_ge(pool_mix, MIX_STEPS * p + 2)
                pool.tensor_tensor(half[:, :], qc[:, 0:4 * I], qc[:, 4 * I:8 * I], ALU.add).then_inc(pool_mix, 1)
                pool.wait_ge(pool_mix, MIX_STEPS * p + 3)
                pool.tensor_tensor(quarter[:, :], half[:, 0:2 * I], half[:, 2 * I:4 * I], ALU.add)\
                    .then_inc(pool_mix, 1)
                pool.wait_ge(pool_mix, MIX_STEPS * p + 4)
                if p >= 1:
                    pool.wait_ge(turned_ready, p)
                pool.tensor_tensor(mixed[:, :], quarter[:, 0:I], quarter[:, I:2 * I], ALU.add)\
                    .then_inc(pool_mix, 1)

            def lo_x(n):
                pool.wait_ge(xhi_ready, n - FIRST + 1)
                pool.tensor_tensor(x_lo[:, n % 2].rearrange("p s b t -> p t s b"),
                                   xT[:, TC * n:TC * (n + 1), :].rearrange("p t (s b) -> p t s b", s=KB),
                                   x_hi[:, n % 2].bitcast(F32).rearrange("p s b t -> p t s b"),
                                   ALU.subtract).then_inc(xlo_ready, 1)

            def lo_gi(n, a):
                pool.wait_ge(gi_hi, gi_index(n, a) + 1)
                part = gi_halves[:, n % 2, 2 * a:2 * a + 2]
                pool.tensor_tensor(part[:, :, HALF + R:HALF + IN], part[:, :, HALF + R:HALF + IN].bitcast(F32),
                                   part[:, :, R:IN].bitcast(F32), ALU.subtract).then_inc(gi_lo, 1)

            def lo_bias(n):
                pool.wait_ge(bias_tok_ready, 3 + n)
                pool.tensor_tensor(gi_halves[:, n, :, HALF:HALF + FJ], bias_tok[:, :, HN:HN + FJ],
                                   gi_halves[:, n, :, HN:HN + FJ].bitcast(F32), ALU.subtract)\
                    .then_inc(bias_lo_ready, 1)

            def lo_piece(i):
                u, s = PIECES[i]
                cols = slice(UW * u, UW * (u + 1))
                pool.wait_ge(w_hi, i + 2)
                pool.tensor_tensor(wlo[:, s, :, cols], wraw[:, s, :, cols], whi[:, s, :, cols].bitcast(F32),
                                   ALU.subtract).then_inc(w_lo_pool, 1)

            def lo_down():
                pool.wait_ge(w_hi, len(PIECES) + 2)
                pool.tensor_tensor(dlo_w[:, :, :], draw[:, :, :], dhi_w[:, :, :].bitcast(F32), ALU.subtract)\
                    .then_inc(w_lo_pool, 1)

            pool.wait_ge(wih_split, 1)
            pool.tensor_tensor(wih_lo[:, 1, :], wih[:, 1, :], wih_hi[:, 1, :].bitcast(F32), ALU.subtract)\
                .then_inc(wih_split, 1)
            for c in range(NC):
                for k in range(TC):
                    halves(TC * c + k)
                    for n, a in gi_due(*after(c, k)):
                        lo_gi(n, a)
                    if (c, k) == (0, 2):
                        lo_piece(1)
                    if (c, k) == (1, 0):
                        lo_bias(0)
                        lo_piece(5)
                        lo_piece(6)
                    if (c, k) == (1, 1):
                        lo_piece(8)
                    if (c, k) == (1, 2):
                        lo_piece(9)
                    for n in x_due(c, k):
                        lo_x(n)
                    if (c, k) == (1, 3):
                        lo_bias(1)
                    if k == 3 and c >= 1:
                        scale_basis(c - 1, 0)
                    if k == 0 and c >= 2:
                        scale_basis(c - 2, 1)
                        add_basis(c - 2)
                    if (c, k) == (2, 1):
                        lo_down()
            scale_basis(LAST - 1, 1)
            add_basis(LAST - 1)
            scaled = q[:, LAST % 2, :]
            pool.wait_ge(q_ready, NU * LAST + 3)
            pool.tensor_tensor(half[:, 0:2 * I], scaled[:, 0:2 * I], scaled[:, 2 * I:4 * I], ALU.add)\
                .then_inc(tail_mix, 1)
            pool.wait_ge(tail_mix, 1)
            pool.wait_ge(q_ready, NU * LAST + 4)
            pool.tensor_tensor(quarter[:, :], half[:, 0:2 * I], scaled[:, 4 * I:6 * I], ALU.add).then_inc(tail_mix, 1)

        @block.scalar
        def _(act):
            act.wait_ge(const_ready, 8)
            act.activation(ident_r[:, :], ident[:, :], ACT.Copy).then_inc(ident_ready, 1)
            for s in range(KB):
                act.wait_ge(ld_wih[s], 16)
            act.activation(wih_hi[:, :, :], wih[:, :, :], ACT.Copy).then_inc(wih_split, 1)

            def hi_x(n):
                act.wait_ge(x_turned, n)
                if n >= FIRST + 2:
                    act.wait_ge(gi_psum, gi_index(n - 2, 1) + 1)
                act.activation(x_hi[:, n % 2].rearrange("p s b t -> p t s b"),
                               xT[:, TC * n:TC * (n + 1), :].rearrange("p t (s b) -> p t s b", s=KB),
                               ACT.Copy).then_inc(xhi_ready, 1)

            def hi_gi(n, a):
                act.wait_ge(gi_biased, gi_index(n, a) + 1)
                part = gi_halves[:, n % 2, 2 * a:2 * a + 2]
                act.activation(part[:, :, R:IN], part[:, :, HALF + R:HALF + IN].bitcast(F32), ACT.Copy)\
                    .then_inc(gi_hi, 1)

            def copy_bias_tok():
                act.wait_ge(bias_tok_psum, 1)
                for a in range(2):
                    act.activation(bias_tok[:, 2 * a:2 * a + 2, :], gi_bank[a][:, :].rearrange("p (j n) -> p j n", j=2),
                                   ACT.Copy).then_inc(bias_tok_ready, 1)

            def hi_bias(n):
                act.wait_ge(bias_tok_ready, 2)
                act.activation(gi_halves[:, n, :, HN:HN + FJ], bias_tok[:, :, HN:HN + FJ], ACT.Copy)\
                    .then_inc(bias_tok_ready, 1)

            def tanh_rz(t):
                act.wait_ge(gates_ready, t + 1)
                act.activation(trz[:, :], gates[t % 2][:, R:R + 2 * FJ], ACT.Tanh, scale=0.5).then_inc(rz_ready, 1)
                act.wait_ge(rz_ready, t + 1)
                act.activation(sc_mul[:, :, 1], trz[:, FJ:2 * FJ], ACT.Copy, bias=0.5, scale=-0.5)\
                    .then_inc(omz_ready, 1)

            def tanh_n(t):
                act.wait_ge(pre_ready, t + 1)
                act.activation(sc_add[:, :, 0], pre[:, :], ACT.Tanh).then_inc(n_ready, 1)

            def hi_router():
                act.wait_ge(ld_router, 16 * KB)
                act.activation(wrouter[:, :, 0, :], rraw[:, :, :], ACT.Copy).then_inc(w_hi, 1)

            def hi_pieces(first, end):
                for u, s in PIECES[first:end]:
                    cols = slice(UW * u, UW * (u + 1))
                    act.wait_ge(ld_routed[s] if u < NU - 1 else ld_shared[s], 16 * 2)
                    act.activation(whi[:, s, :, cols], wraw[:, s, :, cols], ACT.Copy).then_inc(w_hi, 1)

            def hi_down():
                act.wait_ge(ld_down, 32)
                act.activation(dhi_w[:, :, :], draw[:, :, :], ACT.Copy).then_inc(w_hi, 1)

            def tanh_gate(n):
                act.wait_ge(unit_ready, n + 1)
                if n >= 2:
                    act.wait_ge(p1_ready, n - 1)
                act.activation(th[:, n % 2, :], unit_bank[n % NB][:, 0:UW], ACT.Tanh, scale=0.5)\
                    .then_inc(th_ready, 1)

            def softmax_exp(p):
                act.wait_ge(topk_step, TOPK_STEPS * p + 3)
                act.activation(ex[:, :], lx[:, 0:E], ACT.Exp, bias=negmax[:, :], accum_out=exsum[:, :])\
                    .then_inc(ex_ready, 1)

            def copy_emT(p):
                act.wait_ge(emT_turned, p + 1)
                act.activation(emT[:, :], route[:, EMT], ACT.Copy).then_inc(emT_ready, 1)

            def scale_up(u):
                n = NU * LAST + 1 + u
                act.wait_ge(unit_ready, n + 1)
                if u == 0:
                    act.wait_ge(coef_ready, NC)
                    act.wait_ge(pool_mix, MIX_STEPS * (LAST - 1) + 3)
                if u >= 2:
                    act.wait_ge(q_ready, n - 1)
                for k in range(2):
                    last = act.activation(scaled_up[:, u % 2, I * k:I * (k + 1)],
                                          unit_bank[n % NB][:, UW + I * k:UW + I * (k + 1)], ACT.Copy,
                                          scale=coef[:, LAST % 2, 2 * u + k:2 * u + k + 1])
                last.then_inc(up_scaled, 1)

            def hi_turned(p, source, parts, step):
                act.wait_ge(turned_ready, step)
                if p >= 2:
                    act.wait_ge(down_ready, p - 1)
                act.activation(dhi[:, p % 2, parts, :], source[:, 0:3 * P].rearrange("p (a b) -> p a b", a=3)[:, parts],
                               ACT.Copy).then_inc(dhi_ready, 1)

            def slot(c, k):
                p = c - 1

                def input_shares():
                    for n, a in gi_due(*after(c, k)):
                        hi_gi(n, a)
                    for n in x_due(c, k):
                        hi_x(n)

                if c == 0:
                    if k == 0:
                        copy_bias_tok()
                    if k == 1:
                        hi_router()
                        hi_pieces(0, 1)
                    if k == 2:
                        hi_pieces(1, 3)
                    if k == 3:
                        hi_pieces(3, 5)
                        hi_bias(0)
                    input_shares()
                elif k == 0:
                    if p >= 1:
                        tanh_gate(NU * p - 1)
                    else:
                        hi_pieces(5, 7)
                    input_shares()
                elif k == 1:
                    softmax_exp(p)
                    tanh_gate(NU * p)
                    if p == 0:
                        hi_pieces(7, 9)
                    input_shares()
                elif k == 2:
                    tanh_gate(NU * p + 1)
                    copy_emT(p)
                    if p == 0:
                        hi_pieces(9, 10)
                        hi_bias(1)
                    else:
                        hi_turned(p - 1, turned, slice(0, 3), p)
                    input_shares()
                elif k == 3:
                    tanh_gate(NU * p + 2)
                    tanh_gate(NU * p + 3)
                    if p == 0:
                        hi_down()

            for c in range(NC):
                for k in range(TC):
                    t = TC * c + k
                    tanh_rz(t)
                    tanh_n(t)
                    slot(c, k)
            tanh_gate(NU * LAST - 1)
            softmax_exp(LAST)
            tanh_gate(NU * LAST)
            copy_emT(LAST)
            for u in range(NU - 1):
                scale_up(u)
                tanh_gate(NU * LAST + 1 + u)
                if u == 0:
                    hi_turned(LAST, last_turned, slice(1, 3), LAST)
                if u == 1:
                    hi_turned(LAST - 1, turned, slice(0, 3), LAST + 1)
            hi_turned(LAST, last_turned, slice(0, 1), LAST + 2)

        @block.tensor
        def _(pe):
            def x_part(t):
                g = gates[t % 2]
                if t == TC:
                    pe.wait_ge(x_turned, 2)
                for j in range(NJ):
                    which, bias = (pick4[:, j, :], bsum[:, 0, :]) if t == 0 else \
                        (pick[0:2 * Q + NJ, j, :], bias3[0:2 * Q + NJ, :])
                    pe.matmul(g[Q * j:Q * (j + 1), 0:4 * FJ], which, bias,
                              start=True, stop=False, skip_group_check=True)
                for s in range(KB):
                    if t == 0:
                        pe.wait_ge(ld_wih[s], 16)
                    for j in range(NJ):
                        pe.matmul(g[Q * j:Q * (j + 1), R:4 * FJ], xT[:, t, B * s:B * (s + 1)],
                                  wih[:, s, :].rearrange("p (g j c) -> p j g c", g=3, j=NJ)[:, j],
                                  start=False, stop=False, skip_group_check=True)

            def gi_part(n, a):
                dst = gi_bank[a]
                i = gi_index(n, a)
                if i >= 2:
                    pe.wait_ge(gi_biased, i - 1)
                if i == 0:
                    pe.wait_ge(wih_split, 3)
                    pe.wait_ge(bias_tok_ready, 2)
                if a == 0:
                    pe.wait_ge(xlo_ready, n - FIRST + 1)
                c = gi_slot(n, a)[0]
                if c >= 3:
                    pe.wait_ge(out_ready if a else dlo_ready, c - 2)
                for s in range(KB):
                    for m, (st, w) in enumerate(((x_hi, wih_hi), (x_hi, wih_lo), (x_lo, wih_hi))):
                        last = pe.matmul(dst[:, :].rearrange("p (j n) -> p j n", j=2)[:, :, R:4 * FJ],
                                         st[:, n % 2, s, :, :].rearrange("p b t -> p (b t)"),
                                         w[:, s, :].rearrange("p (g j c) -> p j g c", g=3, j=NJ)[:, 2 * a:2 * a + 2],
                                         start=(s == 0 and m == 0), stop=(s == KB - 1 and m == 2))
                last.then_inc(gi_psum, 1)

            def bias_for_tokens():
                pe.wait_ge(bias_step, 11)
                for j in range(NJ):
                    last = pe.matmul(gi_bank[j // 2][:, 4 * FJ * (j % 2):4 * FJ * (j % 2 + 1)],
                                     pick_tok[0:2 * Q + NJ, j, :], bias3[0:2 * Q + NJ, :], start=True, stop=True)
                last.then_inc(bias_tok_psum, 1)

            def inject(t):
                n = t // TC
                if t % TC == 0:
                    pe.wait_ge(gi_loaded[n % RING], 16 * NJ * ((n - FIRST) // RING + 1))
                for a in range(2):
                    pe.matmul(gates[t % 2][:, 0:HALF], ident_r[:, :], gi[:, n % RING, t % TC, HALF * a:HALF * (a + 1)],
                              start=(a == 0), stop=False, skip_group_check=True)

            def h_part(t):
                pe.wait_ge(hT_ready, t + 1)
                g = gates[t % 2]
                for s in range(KB):
                    if t == 0:
                        pe.wait_ge(ld_whh[s], 32)
                    for j in range(NJ):
                        st = hT0[:, B * s:B * (s + 1)] if t == 0 else hT[:, (t - 1) // TC % 2, s, (t - 1) % TC, :]
                        last = pe.matmul(g[Q * j:Q * (j + 1), HN:HN + 3 * FJ], st,
                                         whh[:, s, :].rearrange("p (g j c) -> p j g c", g=3, j=NJ)[:, j],
                                         start=False, stop=(s == KB - 1), skip_group_check=True)
                last.then_inc(gates_ready, 1)

            def three(dst, p, cols, blocks):
                for s in blocks:
                    for n, (st, w) in enumerate(((hThi, whi), (hThi, wlo), (hTlo, whi))):
                        last = pe.matmul(dst, st[:, p % 2, s, :, :].rearrange("p t b -> p (t b)"), w[:, s, :, cols],
                                         start=(s == 0 and n == 0), stop=(s == KB - 1 and n == 2))
                return last

            def logits(p):
                pe.wait_ge(hThi_ready, TC * (p + 1))
                if p == 0:
                    pe.wait_ge(w_lo, 1)
                else:
                    pe.wait_ge(coef_ready, p)
                for s in range(KB):
                    pe.matmul(route[:, LOGITS], hThi[:, p % 2, s, :, :].rearrange("p t b -> p (t b)"),
                              wrouter[:, s, :, :].rearrange("p a e -> p (a e)"),
                              start=(s == 0), stop=False, skip_group_check=True)
                pe.wait_ge(hTlo_ready, TC * (p + 1))
                for s in range(KB):
                    last = pe.matmul(route[:, 0:E], hTlo[:, p % 2, s, :, :].rearrange("p t b -> p (t b)"),
                                     wrouter[:, s, 0, :], start=False, stop=(s == KB - 1), skip_group_check=True)
                last.then_inc(logits_ready, 1)

            def unit(n, blocks):
                p = n // NU
                u = unit_order(p)[n % NU]
                if p == 0:
                    for s in blocks:
                        i = PIECES.index((u, s))
                        if i in LO_VECTOR:
                            pe.wait_ge(w_lo, LO_VECTOR.index(i) + 2)
                        else:
                            pe.wait_ge(w_lo_pool, LO_POOL.index(i) + 1)
                if n >= NB and 0 in blocks:
                    pe.wait_ge(q_ready, n - NB + 1)
                last = three(unit_bank[n % NB][:, :].rearrange("p (g n) -> p g n", g=2), p,
                             slice(UW * u, UW * (u + 1)), blocks)
                if KB - 1 in blocks:
                    last.then_inc(unit_ready, 1)

            def turn_em(p):
                pe.wait_ge(topk_step, TOPK_STEPS * p + 5)
                pe.transpose(route[:, EMT], em[:, :], ident[:, :]).then_inc(emT_turned, 1)

            def coefficients(p):
                if p == 0:
                    pe.wait_ge(mix_step, 6)
                pe.wait_ge(emT_ready, p + 1)
                pe.matmul(route[:, COEF], emT[:, :], mix[:, :], start=True, stop=True).then_inc(coef_psum, 1)

            def turn_hidden(p):
                pe.wait_ge(q_ready, NU * (p + 1))
                pe.wait_ge(pool_mix, MIX_STEPS * (p + 1))
                n = p + 4
                if n < NC:
                    pe.wait_ge(gi_biased, gi_index(n, 0) + 1)
                if p >= 1:
                    pe.wait_ge(dlo_ready, p)
                pe.transpose(turned[:, 0:P], mixed[:, :], ident[:, :])
                pe.transpose(turned[:, P:2 * P], shared[:, p % 2, 0:P], ident[:, :])
                pe.transpose(turned[:, 2 * P:3 * P], shared[:, p % 2, P:2 * P], ident[:, :]).then_inc(turned_ready, 1)

            def project(p):
                n = p + 4
                if n < NC:
                    pe.wait_ge(gi_biased, gi_index(n, 1) + 1)
                if p == 0:
                    pe.wait_ge(w_lo_pool, len(LO_POOL) + 1)
                pe.wait_ge(dlo_ready, p + 1)
                if p >= 1:
                    pe.wait_ge(out_ready, p)
                for a in range(3):
                    for n, (st, w) in enumerate(((dhi, dhi_w), (dhi, dlo_w), (dlo, dhi_w))):
                        last = pe.matmul(down[:, 0:D], st[:, p % 2, a, :], w[:, a, :],
                                         start=(a == 0 and n == 0), stop=(a == 2 and n == 2))
                last.then_inc(down_ready, 1)

            def last_shared_turned():
                pe.wait_ge(q_ready, NU * LAST + 1)
                for a in range(1, 3):
                    last = pe.transpose(last_turned[:, P * a:P * (a + 1)], shared[:, LAST % 2, P * (a - 1):P * a],
                                        ident[:, :])
                last.then_inc(turned_ready, 1)

            def last_shared_projected():
                pe.wait_ge(dlo_last, 1)
                for a in range(1, 3):
                    for n, (st, w) in enumerate(((dhi, dhi_w), (dhi, dlo_w), (dlo, dhi_w))):
                        pe.matmul(last_down[:, 0:D], st[:, LAST % 2, a, :], w[:, a, :],
                                  start=(a == 1 and n == 0), stop=False, skip_group_check=True)

            def last_mixed_turned():
                pe.wait_ge(tail_mix, 2)
                for n, part in enumerate((quarter[:, 0:I], quarter[:, I:2 * I], q[:, LAST % 2, 6 * I:7 * I],
                                          q[:, LAST % 2, 7 * I:8 * I])):
                    if n == 2:
                        pe.wait_ge(q_ready, NU * NC)
                    last = pe.matmul(last_turned[:, 0:P], part, ident[:, :], start=(n == 0), stop=(n == 3))
                last.then_inc(turned_ready, 1)

            def last_mixed_projected():
                pe.wait_ge(dhi_ready, LAST + 2)
                for n, (st, w) in enumerate(((dhi, dhi_w), (dhi, dlo_w), (dlo, dhi_w))):
                    if n == 2:
                        pe.wait_ge(dlo_last, 2)
                    last = pe.matmul(last_down[:, 0:D], st[:, LAST % 2, 0, :], w[:, 0, :],
                                     start=False, stop=(n == 2), skip_group_check=True)
                last.then_inc(down_ready, 1)

            def filler(c, k):
                p = c - 1
                shares = c < NC - 2
                if p >= 0:
                    if k == 0:
                        logits(p)
                        unit(NU * p, range(KB))
                        if not shares:
                            unit(NU * p + 1, [0])
                    if k == 1:
                        unit(NU * p + 1, range(KB) if shares else [1])
                        unit(NU * p + 2, [0] if shares else range(KB))
                    if k == 2:
                        turn_em(p)
                        if shares:
                            unit(NU * p + 2, [1])
                        if p >= 1:
                            turn_hidden(p - 1)
                        unit(NU * p + 3, range(KB))
                        coefficients(p)
                    if k == 3:
                        if p >= 1:
                            project(p - 1)
                        unit(NU * p + 4, range(KB))
                if (c, k) == (0, 0):
                    bias_for_tokens()
                for n, a in gi_due(c, k):
                    gi_part(n, a)

            pe.wait_ge(empty_ready, 1)
            for _ in range(WARM):
                pe.matmul(route[:, 0:2 * P], empty[:, 0:P], empty[:, :], start=True, stop=True)
            pe.wait_ge(const_ready, 1)
            pe.wait_ge(bias_step, 3)
            pe.wait_ge(x_turned, 1)
            x_part(0)
            pe.wait_ge(ident_ready, 1)
            pe.wait_ge(bias_step, 11)
            for c in range(NC):
                for k in range(TC):
                    t = TC * c + k
                    h_part(t)
                    if t + 1 < TC * FIRST:
                        x_part(t + 1)
                    elif t + 1 < T:
                        inject(t + 1)
                    filler(c, k)
            n = NU * LAST
            logits(LAST)
            unit(n, range(KB))
            unit(n + 1, range(KB))
            turn_em(LAST)
            unit(n + 2, [0])
            coefficients(LAST)
            last_shared_turned()
            unit(n + 2, [1])
            turn_hidden(LAST - 1)
            unit(n + 3, range(KB))
            unit(n + 4, range(KB))
            last_shared_projected()
            project(LAST - 1)
            last_mixed_turned()
            last_mixed_projected()

        @block.vector
        def _(dve):
            dve.memset(empty[:, :], 0.0).then_inc(empty_ready, 1)
            for zeros in (pick4, pick, pick_tok):
                dve.memset(zeros[:, :, :], 0.0).then_inc(zeroed, 1)
            dve.memset(ident[:, :], 0.0).then_inc(zeroed, 1)
            dve.memset(bias3[:, :], 0.0).then_inc(zeroed, 1)
            dve.memset(sc_mul[:, :, :], 0.0).then_inc(zeroed, 1)
            dve.memset(lx[:, E:E + TOPK], LOWEST).then_inc(zeroed, 1)
            dve.memset(keys[:, TOPK:8], LOWEST).then_inc(zeroed, 1)
            dve.wait_ge(ld_bias, 32)
            dve.tensor_copy(bsum[:, 0, HN:HN + FJ], bh4[:, 2, :]).then_inc(bias_step, 1)
            dve.tensor_tensor(bsum[:, 0, R:R + 2 * FJ].rearrange("j (g c) -> j g c", g=2),
                              bi4[:, 0:2, :], bh4[:, 0:2, :], ALU.add).then_inc(bias_step, 1)
            dve.tensor_copy(bsum[:, 0, IN:IN + FJ], bi4[:, 2, :]).then_inc(bias_step, 1)
            dve.wait_ge(bias_step, 3)
            dve.wait_ge(zeroed, 8)
            dve.wait_ge(ld_x0, 16 * NJ)
            dve.transpose(xT[:, 0:TC, :].rearrange("p t f -> p (t f)"),
                          xj[:, 0:TC, :].rearrange("p t f -> p (t f)")).then_inc(x_turned, 1)
            dve.wait_ge(ld_h0, 16)
            dve.transpose(hT0[:, :], h0[:, :]).then_inc(hT_ready, 1)
            dve.tensor_scalar(hhalf[:, :], h0[:, :], 0.5, None, ALU.mult).then_inc(hhalf_ready, 1)
            for a in range(3):
                dve.tensor_copy(bpart[:, a, :], bsum[:, a, :]).then_inc(bias_step, 1)
                dve.wait_ge(bias_step, 4 + 3 * a)
                dve.tensor_copy(bias3[Q * a:Q * a + NJ, :], bpart[:, a, :]).then_inc(bias_step, 1)
                if a < 2:
                    dve.tensor_tensor(bsum[:, a + 1, :], bsum[:, a, :], bpart[:, a, :], ALU.subtract)\
                        .then_inc(bias_step, 1)
                    dve.wait_ge(bias_step, 6 + 3 * a)

            def gru_step(t):
                c, k = t // TC, t % TC
                g = gates[t % 2]
                dve.wait_ge(rz_ready, t + 1)
                dve.scalar_tensor_tensor(out=m[:, :], in0=trz[:, 0:FJ], scalar=1.0, in1=g[:, HN:HN + FJ],
                                         op0=ALU.add, op1=ALU.mult).then_inc(m_ready, 1)
                dve.wait_ge(m_ready, t + 1)
                share = g[:, IN:IN + FJ] if c < FIRST else gi[:, c % RING, k, 2 * HALF:GI].bitcast(F32)
                dve.scalar_tensor_tensor(out=pre[:, :], in0=m[:, :], scalar=0.5, in1=share,
                                         op0=ALU.mult, op1=ALU.add).then_inc(pre_ready, 1)
                dve.wait_ge(hhalf_ready, t + 1)
                dve.scalar_tensor_tensor(out=sc_add[:, :, 1], in0=trz[:, FJ:2 * FJ], scalar=1.0, in1=hhalf[:, :],
                                         op0=ALU.add, op1=ALU.mult).then_inc(blend_ready, 1)
                dve.wait_ge(blend_ready, t + 1)
                dve.wait_ge(n_ready, t + 1)
                dve.tensor_tensor_scan(sc_out[:, :, :].rearrange("p f a -> p (f a)"),
                                       sc_mul[:, :, :].rearrange("p f a -> p (f a)"),
                                       sc_add[:, :, :].rearrange("p f a -> p (f a)"),
                                       0.0, ALU.mult, ALU.add).then_inc(h_ready, 1)
                dve.wait_ge(h_ready, t + 1)
                if k == 0 and c >= 2:
                    dve.wait_ge(hTlo_ready, TC * (c - 1))
                dve.transpose(hT[:, c % 2, :, k, :], sc_out[:, :, 1]).then_inc(hT_ready, 1)
                dve.tensor_scalar(hhalf[:, :], sc_out[:, :, 1], 0.5, None, ALU.mult).then_inc(hhalf_ready, 1)

            def turn_x(t0, t1, loaded):
                dve.wait_ge(loaded, 16 * NJ)
                dve.transpose(xT[:, t0:t1, :].rearrange("p t f -> p (t f)"),
                              xj[:, t0:t1, :].rearrange("p t f -> p (t f)")).then_inc(x_turned, 1)

            def lo_router():
                dve.wait_ge(w_hi, 1)
                dve.tensor_tensor(wrouter[:, :, 1, :], rraw[:, :, :],
                                  wrouter[:, :, 0, :].bitcast(F32), ALU.subtract).then_inc(w_lo, 1)

            def lo_piece(i):
                u, s = PIECES[i]
                cols = slice(UW * u, UW * (u + 1))
                dve.wait_ge(w_hi, i + 2)
                dve.tensor_tensor(wlo[:, s, :, cols], wraw[:, s, :, cols], whi[:, s, :, cols].bitcast(F32),
                                  ALU.subtract).then_inc(w_lo, 1)

            def mixing_table(step):
                if step == 0:
                    dve.wait_ge(ld_mix, 32)
                else:
                    dve.wait_ge(mix_step, step)
                if step == 0:
                    dve.tensor_tensor(amp2[:, :, :], amp[:, :, :], amp[:, :, :], ALU.mult).then_inc(mix_step, 1)
                elif step == 1:
                    dve.tensor_tensor(pk[:, :], amp2[:, :, 0], amp2[:, :, 1], ALU.add).then_inc(mix_step, 1)
                elif step == 2:
                    dve.tensor_reduce(psum_k[:, :], pk[:, :], mybir.AxisListType.X, ALU.add).then_inc(mix_step, 1)
                elif step == 3:
                    dve.tensor_scalar(prec[:, :], psum_k[:, :], EPS, None, ALU.add).then_inc(mix_step, 1)
                elif step == 4:
                    dve.reciprocal(prec[:, :], prec[:, :]).then_inc(mix_step, 1)
                else:
                    dve.tensor_scalar(mix[:, :], pk[:, :], prec[:, :], scale_e[:, :], ALU.mult, ALU.mult)\
                        .then_inc(mix_step, 1)

            def gated_p1(n):
                dve.wait_ge(th_ready, n + 1)
                if n >= 2:
                    dve.wait_ge(q_ready, n - 1)
                dve.scalar_tensor_tensor(out=p1[:, n % 2, :], in0=th[:, n % 2, :], scalar=1.0,
                                         in1=unit_bank[n % NB][:, 0:UW], op0=ALU.add, op1=ALU.mult)\
                    .then_inc(p1_ready, 1)

            def gated_q(n):
                p = n // NU
                u = unit_order(p)[n % NU]
                dve.wait_ge(p1_ready, n + 1)
                if n % NU == 0 and p >= 2:
                    dve.wait_ge(pool_mix, MIX_STEPS * (p - 2) + 2)
                dst = q[:, p % 2, UW * u:UW * (u + 1)] if u < NU - 1 else shared[:, p % 2, :]
                dve.scalar_tensor_tensor(out=dst, in0=p1[:, n % 2, :], scalar=0.5, in1=unit_bank[n % NB][:, UW:2 * UW],
                                         op0=ALU.mult, op1=ALU.mult).then_inc(q_ready, 1)

            def scaled_q(u):
                n = NU * LAST + 1 + u
                dve.wait_ge(p1_ready, n + 1)
                dve.wait_ge(up_scaled, u + 1)
                dve.tensor_tensor(q[:, LAST % 2, UW * u:UW * (u + 1)], p1[:, n % 2, :], scaled_up[:, u % 2, :],
                                  ALU.mult).then_inc(q_ready, 1)

            def bias_gi(n, a):
                i = gi_index(n, a)
                dve.wait_ge(gi_psum, i + 1)
                if n >= FIRST + 2 and a == 0:
                    dve.wait_ge(gi_loaded[n % RING], 16 * NJ * ((n - FIRST) // RING))
                dve.tensor_tensor(gi_halves[:, n % 2, 2 * a:2 * a + 2, HALF + R:GI].bitcast(F32),
                                  gi_bank[a][:, :].rearrange("p (j n) -> p j n", j=2)[:, :, R:4 * FJ],
                                  bias_tok[:, 2 * a:2 * a + 2, R:4 * FJ], ALU.add).then_inc(gi_biased, 1)

            def copy_logits(p):
                dve.wait_ge(logits_ready, p + 1)
                dve.tensor_reduce(lx[:, 0:E], route[:, LOGITS].rearrange("p (a e) -> p e a", a=2), mybir.AxisListType.X,
                                  ALU.add).then_inc(lx_ready, 1)

            def topk_max(p):
                dve.wait_ge(lx_ready, p + 1)
                dve.max(v8[:, :], lx[:, 0:E]).then_inc(topk_step, 1)

            def topk_keys(p):
                dve.wait_ge(topk_step, TOPK_STEPS * p + 1)
                dve.tensor_scalar(negmax[:, :], v8[:, 0:1], -1.0, None, ALU.mult).then_inc(topk_step, 1)
                dve.tensor_copy(keys[:, 0:TOPK], v8[:, 0:TOPK]).then_inc(topk_step, 1)

            def topk_mark(p):
                dve.wait_ge(topk_step, TOPK_STEPS * p + 3)
                dve.match_replace(out=marked[:, :], in_to_replace=keys[:, :], in_values=lx[:, :],
                                  imm_value=HIGHEST).then_inc(topk_step, 1)

            def topk_em(p):
                dve.wait_ge(topk_step, TOPK_STEPS * p + 4)
                dve.wait_ge(ex_ready, p + 1)
                dve.scalar_tensor_tensor(out=em[:, :], in0=marked[:, 0:E], scalar=HIGHEST, in1=ex[:, :],
                                         op0=ALU.is_equal, op1=ALU.mult, accum_out=sum4[:, :]).then_inc(topk_step, 1)

            def topk_den(p):
                dve.wait_ge(topk_step, TOPK_STEPS * p + 5)
                dve.scalar_tensor_tensor(out=den[:, :], in0=exsum[:, :], scalar=EPS, in1=sum4[:, :],
                                         op0=ALU.mult, op1=ALU.add).then_inc(topk_step, 1)

            def topk_rec(p):
                dve.wait_ge(topk_step, TOPK_STEPS * p + 6)
                dve.reciprocal(rec[:, :], den[:, :]).then_inc(topk_step, 1)

            def scale_coefficients(p):
                dve.wait_ge(topk_step, TOPK_STEPS * (p + 1))
                dve.wait_ge(coef_psum, p + 1)
                dve.tensor_scalar(coef[:, p % 2, :], route[:, COEF], rec[:, :], 0.5 if p == LAST else 1.0,
                                  ALU.mult, ALU.mult).then_inc(coef_ready, 1)

            def lo_turned(p, source, parts, step):
                dve.wait_ge(dhi_ready, step)
                dve.tensor_tensor(dlo[:, p % 2, parts, :],
                                  source[:, 0:3 * P].rearrange("p (a b) -> p a b", a=3)[:, parts],
                                  dhi[:, p % 2, parts, :].bitcast(F32), ALU.subtract)\
                    .then_inc(dlo_ready if p < LAST else dlo_last, 1)

            def residual(p, source):
                dve.wait_ge(down_ready, p + 1)
                if p == 0:
                    dve.wait_ge(ld_xtok, 16 * TC)
                if p >= 2:
                    dve.wait_ge(stored[p % 2], 16 * (p // 2))
                dve.tensor_tensor(ot[:, p % 2, :], source[:, 0:D], xtok[:, p, :], ALU.add).then_inc(out_ready, 1)

            def slot(c, k):
                p = c - 1
                for n, a in gi_due(*after(c, k)):
                    bias_gi(n, a)
                for n in x_due(c, k):
                    if n >= FIRST + 2:
                        turn_x(TC * n, TC * (n + 1), ld_x2)
                if c == 0:
                    if k == 0:
                        turn_x(TC, 3 * TC, ld_x1)
                        dve.wait_ge(wih_split, 1)
                        dve.tensor_tensor(wih_lo[:, 0, :], wih[:, 0, :], wih_hi[:, 0, :].bitcast(F32), ALU.subtract)\
                            .then_inc(wih_split, 1)
                    if k == 1:
                        turn_x(3 * TC, 4 * TC, ld_x1)
                        lo_router()
                        lo_piece(0)
                    if k == 2:
                        lo_piece(2)
                    if k == 3:
                        lo_piece(3)
                        lo_piece(4)
                elif k == 0:
                    copy_logits(p)
                    if p == 0:
                        mixing_table(0)
                    topk_max(p)
                    if p == 0:
                        mixing_table(1)
                        mixing_table(2)
                    topk_keys(p)
                    if p >= 1:
                        gated_p1(NU * p - 1)
                    topk_mark(p)
                    if p >= 1:
                        gated_q(NU * p - 1)
                elif k == 1:
                    topk_em(p)
                    if p == 0:
                        mixing_table(3)
                    gated_p1(NU * p)
                    if p == 0:
                        mixing_table(4)
                    topk_den(p)
                    gated_q(NU * p)
                    topk_rec(p)
                    if p == 0:
                        mixing_table(5)
                        lo_piece(7)
                elif k == 2:
                    gated_p1(NU * p + 1)
                    if p >= 1:
                        lo_turned(p - 1, turned, slice(0, 3), p)
                    gated_q(NU * p + 1)
                    scale_coefficients(p)
                elif k == 3:
                    gated_p1(NU * p + 2)
                    gated_p1(NU * p + 3)
                    gated_q(NU * p + 2)
                    gated_q(NU * p + 3)
                    if 1 <= p < LAST - 1:
                        residual(p - 1, down)

            for c in range(NC):
                for k in range(TC):
                    gru_step(TC * c + k)
                    slot(c, k)
            n = NU * LAST
            copy_logits(LAST)
            topk_max(LAST)
            topk_keys(LAST)
            gated_p1(n - 1)
            topk_mark(LAST)
            gated_q(n - 1)
            topk_em(LAST)
            topk_den(LAST)
            gated_p1(n)
            topk_rec(LAST)
            gated_q(n)
            residual(LAST - 2, down)
            scale_coefficients(LAST)
            for u in range(NU - 1):
                gated_p1(n + 1 + u)
                scaled_q(u)
                if u == 0:
                    lo_turned(LAST, last_turned, slice(1, 3), LAST)
                if u == 1:
                    lo_turned(LAST - 1, turned, slice(0, 3), LAST + 1)
            residual(LAST - 1, down)
            lo_turned(LAST, last_turned, slice(0, 1), LAST + 2)
            residual(LAST, last_down)


_INS = ['x', 'cond_2048', 'L0_cond_W_ih', 'L0_cond_W_hh', 'L0_cond_b_ih', 'L0_cond_b_hh', 'L0_ffn_w_router',
        'L0_ffn_w_gate', 'L0_ffn_w_up', 'L0_ffn_w_down', 'L0_ffn_amplitudes', 'L0_ffn_expert_scale',
        'L0_ffn_shared_w_gate', 'L0_ffn_shared_w_up', 'L0_ffn_shared_w_down']
_OUT = ((B, T, D), 'float32')


def kernel(**inputs):
    import numpy as _np
    import concourse.bacc as _bacc
    from concourse import mybir as _mybir
    from concourse.bass_utils import run_bass_kernel_spmd as _run

    nc = _bacc.Bacc("TRN2", target_bir_lowering=False, num_devices=1)
    arrays, args = {}, []
    for name in _INS:
        a = _np.ascontiguousarray(inputs[name])
        arrays[f"in_{name}_dram"] = a
        args.append(nc.dram_tensor(f"in_{name}_dram", a.shape, _mybir.dt.from_np(a.dtype), kind="ExternalInput").ap())
    shape, dtype = _OUT
    out = nc.dram_tensor("out_0_dram", shape, _mybir.dt.from_np(_np.dtype(dtype)), kind="ExternalOutput").ap()
    build(nc, *args, out)
    r = _run(nc, [arrays], core_ids=[0])
    return r.results[0]["out_0_dram"]
```
